# Optimizing a Trainium2 kernel written in Bass

```python
import numpy as np
import jax
import jax.numpy as jnp

def _softmax(x, axis=-1):
    return jax.nn.softmax(x, axis=axis)

def _gelu(x):
    return jax.nn.gelu(x, approximate=True)

def _silu(x):
    return jax.nn.silu(x)

def _sigmoid(x):
    return jax.nn.sigmoid(x)

def _layernorm(x, axis=-1, eps=1e-05):
    m = jnp.mean(x, axis=axis, keepdims=True)
    v = jnp.var(x, axis=axis, keepdims=True)
    return (x - m) / jnp.sqrt(v + eps)

def _scatter_add(tgt, idx, src, axis=0):
    return tgt.at[idx].add(src)

def _segment_sum(src, seg, n):
    return jax.ops.segment_sum(src, seg, n)
kernel_name = 'mk_prb_d1_jaxref_r4_14a4fa'

def setup_inputs(seed: int=0):
    np.random.seed(seed)
    _w = jnp.asarray

    def _L0_attn_setup():
        import math
        import jax, jax.numpy as jnp
        import numpy as np
        D_MODEL = 256
        D_STATE = 16
        D_CONV = 4
        EXPAND = 2
        D_INNER = D_MODEL * EXPAND
        B_SZ = 2
        L_SEQ = 512
        DT_MIN = 0.001
        DT_MAX = 0.1

        def _silu(v):
            return v * jax.nn.sigmoid(v)

        def _mamba(x, in_proj_w, conv_w, conv_b, x_proj_w, dt_proj_w, dt_proj_b, A_log, D, out_proj_w):
            xz = jnp.einsum('bld,ed->ble', x, in_proj_w)
            x_in, z = jnp.split(xz, 2, axis=-1)
            xc = jnp.swapaxes(x_in, 1, 2)
            xc = jax.lax.conv_general_dilated(xc, conv_w, window_strides=(1,), padding=[(D_CONV - 1, 0)], dimension_numbers=('NCH', 'OIH', 'NCH'), feature_group_count=D_INNER)
            xc = xc + conv_b[None, :, None]
            x_in = _silu(jnp.swapaxes(xc, 1, 2))
            dbc = jnp.einsum('bld,ed->ble', x_in, x_proj_w)
            delta_in = dbc[..., :D_INNER]
            Bp = dbc[..., D_INNER:D_INNER + D_STATE]
            Cp = dbc[..., D_INNER + D_STATE:]
            delta = jax.nn.softplus(jnp.einsum('bld,ed->ble', delta_in, dt_proj_w) + dt_proj_b)
            A = -jnp.exp(A_log)

            def step(h, inp):
                dt, bt, ct, xt = inp
                dA = jnp.exp(dt[:, :, None] * A[None])
                h = dA * h + dt[:, :, None] * bt[:, None, :] * xt[:, :, None]
                y = jnp.einsum('bds,bs->bd', h, ct) + D * xt
                return (h, y)
            tm = lambda a: jnp.swapaxes(a, 0, 1)
            h0 = jnp.zeros((x.shape[0], D_INNER, D_STATE), x.dtype)
            _, y = jax.lax.scan(step, h0, (tm(delta), tm(Bp), tm(Cp), tm(x_in)))
            y = jnp.swapaxes(y, 0, 1)
            return jnp.einsum('ble,de->bld', y * _silu(z), out_proj_w)
        key = jax.random.key(seed)
        ks = jax.random.split(key, 8)

        def lin(k, out_f, in_f):
            return jax.random.normal(k, (out_f, in_f), jnp.float32) / np.sqrt(in_f)
        x = jax.random.normal(ks[0], (B_SZ, L_SEQ, D_MODEL), jnp.float32)
        in_proj_w = lin(ks[1], 2 * D_INNER, D_MODEL)
        conv_w = jax.random.normal(ks[2], (D_INNER, 1, D_CONV), jnp.float32) / np.sqrt(D_CONV)
        conv_b = jnp.zeros((D_INNER,), jnp.float32)
        x_proj_w = lin(ks[3], 2 * D_STATE + D_INNER, D_INNER)
        dt_proj_w = lin(ks[4], D_INNER, D_INNER)
        dt = jnp.exp(jax.random.uniform(ks[5], (D_INNER,), jnp.float32) * (math.log(DT_MAX) - math.log(DT_MIN)) + math.log(DT_MIN))
        dt_proj_b = dt + jnp.log(-jnp.expm1(-dt))
        A_log = jnp.log(jnp.tile(jnp.arange(1, D_STATE + 1, dtype=jnp.float32), (D_INNER, 1)))
        D = jnp.ones((D_INNER,), jnp.float32)
        out_proj_w = lin(ks[6], D_MODEL, D_INNER)
        return dict(x=x, in_proj_w=in_proj_w, conv_w=conv_w, conv_b=conv_b, x_proj_w=x_proj_w, dt_proj_w=dt_proj_w, dt_proj_b=dt_proj_b, A_log=A_log, D=D, out_proj_w=out_proj_w)
    _L0_attn_in = _L0_attn_setup()

    def _L0_ffn_setup():
        import jax, jax.numpy as jnp
        import numpy as np
        TOP_K = 2
        key = jax.random.key(seed)
        k1, k2, k3, k4 = jax.random.split(key, 4)
        B, N, D, E, F = (4, 512, 256, 8, 1024)
        x = jax.random.normal(k1, (B, N, D), dtype=jnp.float32)
        gate_w = jax.random.normal(k2, (D, E), dtype=jnp.float32) * D ** (-0.5)
        w1 = jax.random.normal(k3, (E, D, F), dtype=jnp.float32) * D ** (-0.5)
        w2 = jax.random.normal(k4, (E, F, D), dtype=jnp.float32) * F ** (-0.5)
        return {'x': x, 'gate_w': gate_w, 'w1': w1, 'w2': w2}
    _L0_ffn_in = _L0_ffn_setup()
    _d = {'L0_attn_x': _L0_attn_in['x'], 'L0_attn_in_proj_w': _L0_attn_in['in_proj_w'], 'L0_attn_conv_w': _L0_attn_in['conv_w'], 'L0_attn_conv_b': _L0_attn_in['conv_b'], 'L0_attn_x_proj_w': _L0_attn_in['x_proj_w'], 'L0_attn_dt_proj_w': _L0_attn_in['dt_proj_w'], 'L0_attn_dt_proj_b': _L0_attn_in['dt_proj_b'], 'L0_attn_A_log': _L0_attn_in['A_log'], 'L0_attn_D': _L0_attn_in['D'], 'L0_attn_out_proj_w': _L0_attn_in['out_proj_w'], 'L0_ffn_gate_w': _L0_ffn_in['gate_w'], 'L0_ffn_w1': _L0_ffn_in['w1'], 'L0_ffn_w2': _L0_ffn_in['w2']}
    _x0 = _d['L0_attn_x']
    _d['L0_attn_x'] = jax.random.normal(jax.random.fold_in(jax.random.key(seed), 1), (1, 4096, 256), dtype=_x0.dtype)
    del _x0
    return _d

def reference(L0_attn_x, L0_attn_in_proj_w, L0_attn_conv_w, L0_attn_conv_b, L0_attn_x_proj_w, L0_attn_dt_proj_w, L0_attn_dt_proj_b, L0_attn_A_log, L0_attn_D, L0_attn_out_proj_w, L0_ffn_gate_w, L0_ffn_w1, L0_ffn_w2):

    def _L0_attn_ref(x, in_proj_w, conv_w, conv_b, x_proj_w, dt_proj_w, dt_proj_b, A_log, D, out_proj_w):
        import math
        import jax, jax.numpy as jnp
        import numpy as np
        D_MODEL = 256
        D_STATE = 16
        D_CONV = 4
        EXPAND = 2
        D_INNER = D_MODEL * EXPAND
        B_SZ = 2
        L_SEQ = 512
        DT_MIN = 0.001
        DT_MAX = 0.1

        def _silu(v):
            return v * jax.nn.sigmoid(v)

        def _mamba(x, in_proj_w, conv_w, conv_b, x_proj_w, dt_proj_w, dt_proj_b, A_log, D, out_proj_w):
            xz = jnp.einsum('bld,ed->ble', x, in_proj_w)
            x_in, z = jnp.split(xz, 2, axis=-1)
            xc = jnp.swapaxes(x_in, 1, 2)
            xc = jax.lax.conv_general_dilated(xc, conv_w, window_strides=(1,), padding=[(D_CONV - 1, 0)], dimension_numbers=('NCH', 'OIH', 'NCH'), feature_group_count=D_INNER)
            xc = xc + conv_b[None, :, None]
            x_in = _silu(jnp.swapaxes(xc, 1, 2))
            dbc = jnp.einsum('bld,ed->ble', x_in, x_proj_w)
            delta_in = dbc[..., :D_INNER]
            Bp = dbc[..., D_INNER:D_INNER + D_STATE]
            Cp = dbc[..., D_INNER + D_STATE:]
            delta = jax.nn.softplus(jnp.einsum('bld,ed->ble', delta_in, dt_proj_w) + dt_proj_b)
            A = -jnp.exp(A_log)

            def step(h, inp):
                dt, bt, ct, xt = inp
                dA = jnp.exp(dt[:, :, None] * A[None])
                h = dA * h + dt[:, :, None] * bt[:, None, :] * xt[:, :, None]
                y = jnp.einsum('bds,bs->bd', h, ct) + D * xt
                return (h, y)
            tm = lambda a: jnp.swapaxes(a, 0, 1)
            h0 = jnp.zeros((x.shape[0], D_INNER, D_STATE), x.dtype)
            _, y = jax.lax.scan(step, h0, (tm(delta), tm(Bp), tm(Cp), tm(x_in)))
            y = jnp.swapaxes(y, 0, 1)
            return jnp.einsum('ble,de->bld', y * _silu(z), out_proj_w)
        return _mamba(x, in_proj_w, conv_w, conv_b, x_proj_w, dt_proj_w, dt_proj_b, A_log, D, out_proj_w)

    def _L0_ffn_ref(x, gate_w, w1, w2):
        import jax, jax.numpy as jnp
        import numpy as np
        TOP_K = 2
        E = gate_w.shape[-1]
        gate_logits = jnp.einsum('bnd,de->bne', x, gate_w)
        gate_probs = jax.nn.softmax(gate_logits, axis=-1)
        top_k_probs, top_k_idx = jax.lax.top_k(gate_probs, TOP_K)
        top_k_weights = top_k_probs / jnp.sum(top_k_probs, axis=-1, keepdims=True)
        comb = jnp.sum(jax.nn.one_hot(top_k_idx, E, dtype=x.dtype) * top_k_weights[..., None], axis=2)
        h = jax.nn.gelu(jnp.einsum('bnd,edf->benf', x, w1))
        expert_out = jnp.einsum('benf,efd->bend', h, w2)
        output = jnp.einsum('bne,bend->bnd', comb, expert_out)
        return output
    x = L0_attn_x
    xn = _layernorm(x, axis=-1)
    x = x + _L0_attn_ref(xn, L0_attn_in_proj_w, L0_attn_conv_w, L0_attn_conv_b, L0_attn_x_proj_w, L0_attn_dt_proj_w, L0_attn_dt_proj_b, L0_attn_A_log, L0_attn_D, L0_attn_out_proj_w) + _L0_ffn_ref(xn, L0_ffn_gate_w, L0_ffn_w1, L0_ffn_w2)
    return x

_drawn_inputs = setup_inputs


def setup_inputs(seed=0):
    import zlib

    import numpy as np

    out = dict(_drawn_inputs(seed))
    spreads = {'L0_attn_conv_b': (0.0, 0.1), 'L0_attn_D': (1.0, 0.2)}
    factors = {}
    for name, (base, spread) in spreads.items():
        noise = np.random.default_rng([zlib.crc32(name.encode()), seed]).standard_normal(out[name].shape)
        drawn = base * np.exp(spread * noise) if base else spread * noise
        out[name] = jnp.asarray(drawn.astype(out[name].dtype))
    for name, factor in factors.items():
        out[name] = (out[name] * factor).astype(out[name].dtype)
    return out
```

```python
from contextlib import ExitStack

import numpy as np

import concourse.bass as bass
from concourse import mybir

ALU = mybir.AluOpType
ACT = mybir.ActivationFunctionType
F32 = mybir.dt.float32
F32R = mybir.dt.float32r
I32 = mybir.dt.int32
AX_X = mybir.AxisListType.X

P = 128
L = 4096
D = 256
KD = D // P
DI = 512
CT = DI // P
S = 16
TAPS = 4
T = 256
NCH = L // T
TT = T // P
NT = L // P
SQ = 4
NQ = S // SQ
STEPS = CT * NQ
E = 8
F = 1024
FT = F // P
HF = F // 2
SLOTS = 72
GROUPS = NCH // 2
GS = 2 * STEPS
GM = SLOTS // GROUPS
BLOCK_AT = [m * GS // GM for m in range(GM)]
EPS = 1e-5
SP_CUT = 30.0

PJ_X, PJ_OUT, PJ_Z, PJ_DT, PJ_BC, PJ_SPREAD = 8, 10, 11, 13, 15, 16
PJ_HEAD = 15


def pj_index(J, r):
    if isinstance(J, int) and J == 0 and r < PJ_OUT:
        return PJ_HEAD + r
    if isinstance(J, int) and J >= NCH - 1 and r == PJ_OUT:
        return PJ_HEAD - 1 + 24 * (NCH - 1) + PJ_X + J - (NCH - 1)
    return PJ_HEAD - 1 + 24 * J + r


def pj_ahead(J, r):
    if isinstance(J, int) and J == 0:
        return {PJ_X: 0, PJ_X + 1: 1, PJ_Z: 2, PJ_Z + 1: 3, PJ_DT: 4, PJ_DT + 1: 5, PJ_BC: 6}.get(r, r - PJ_SPREAD + 7)
    return pj_index(J - 1, r)


def spread_use(J, q, i):
    if q < 2:
        return pj_ahead(J, PJ_SPREAD + 4 * q + i)
    return pj_index(J, 4 * (q - 2) + i)


def wait(eng, sem, value):
    if isinstance(value, int) and value <= 0:
        return
    eng.wait_ge(sem, value)


def mamba_moe_kernel(nc, x, in_wT, conv_w, conv_b, xp_w, bc_wT, dt_wT, dt_b, A_log, D_skip, out_wT,
                     gate_w, w1, w2, out):
    with ExitStack() as ctx:
        def sb(name, shape, dt=F32):
            return ctx.enter_context(nc.sbuf_tensor(name, shape, dt))

        def sem(name):
            return ctx.enter_context(nc.semaphore(name))

        xnT_d = nc.dram_tensor("xnT_d", [NCH, P, KD * T], F32, kind="Internal").ap()
        rows_d = nc.dram_tensor("rows_d", [SLOTS * P, D], F32, kind="Internal").ap()
        yrows_d = nc.dram_tensor("yrows_d", [SLOTS * P, D], F32, kind="Internal").ap()
        mix_d = nc.dram_tensor("mix_d", [L, D], F32, kind="Internal").ap()

        w2s = sb("w2s", [P, E * FT * D])
        w1s = sb("w1s", [P, 3, KD, HF])
        w_in = sb("w_in", [P, KD, 2 * DI])
        w_dt = sb("w_dt", [P, CT, DI])
        w_bc = sb("w_bc", [P, CT, P])
        w_out = sb("w_out", [P, CT, D])
        ident = sb("ident", [P, P])
        pick = sb("pick", [P, 2 * S], F32R)
        a_neg = sb("a_neg", [P, CT, S])
        cw = sb("cw", [P, CT, TAPS])
        cb = sb("cb", [P, CT])
        dtb = sb("dtb", [P, CT])
        dskip = sb("dskip", [P, CT])
        gw = sb("gw", [P, KD, E])

        bc = sb("bc", [P, 2, S, T])
        xnT = sb("xnT", [P, KD, T])
        xres = sb("xres", [P, TT, D])
        xraw = sb("xraw", [P, CT, TAPS - 1 + T])
        xc = sb("xc", [P, CT, T])
        xin = sb("xin", [P, 2, CT, T])
        delta = sb("delta", [P, 2, CT, T])
        dx = sb("dx", [P, 2, CT, T])
        gz = sb("gz", [P, 2, CT, T])
        u = sb("u", [P, 2, SQ * T])
        prod = sb("prod", [P, 2, SQ * T])
        half = sb("half", [P, 2, SQ * T // 2])
        carry = sb("carry", [P, CT, S])
        bcr = sb("bcr", [P, T], F32R)

        xs = sb("xs", [P, 3, D])
        xsT = sb("xsT", [P, KD, P])
        hT = sb("hT", [P, FT, P])

        pos = sb("pos", [P, 2, NT], I32)
        wgt = sb("wgt", [P, 2, NT])
        slot_e = sb("slot_e", [P, SLOTS], I32)

        xn_all = bc.rearrange("p a s t -> p (a s) t")
        xw_tmp = delta.rearrange("p a c t -> p (a c t)").rearrange("p (c j) -> p c j", c=CT)
        dtw_tmp = dx.rearrange("p a c t -> p (a c t)").rearrange("p (c j) -> p c j", c=CT)
        xnT_tmp = gz.rearrange("p a c t -> p (a c) t")
        stage = u.rearrange("p a n -> p (a n)")
        stage2 = prod.rearrange("p a n -> p (a n)")
        zeros = xin.rearrange("p a c t -> p (a c t)")
        upper = half[:, 0, 0:P]
        ones = half[:, 0, P:2 * P]
        stats = stage2[:, 1024:1024 + 6 * NT].rearrange("p (n k) -> p n k", k=6)
        mv = stage2[:, 1280:1280 + 2 * NT].rearrange("p (n k) -> p n k", k=2)
        rstd = stage2[:, 1408:1408 + NT]
        pickf = half[:, 1, 64:96]
        em8i = half[:, 1, 96:104].bitcast(I32)
        em8 = half[:, 1, 104:112]
        sloti = half[:, 1, 112:112 + SLOTS].bitcast(I32)
        slotf = half[:, 1, 192:192 + SLOTS]
        small = [half[:, 1, 272 + 32 * i:304 + 32 * i] for i in range(6)]
        e8 = [half[:, 1, 464 + 8 * i:472 + 8 * i] for i in range(6)]

        hs = ctx.enter_context(nc.psum_tensor("hs", [P, 2, SQ * T], F32))
        ysum = ctx.enter_context(nc.psum_tensor("ysum", [P, 512], F32))
        pj = ctx.enter_context(nc.psum_tensor("pj", [P, 512], F32))
        m0 = ctx.enter_context(nc.psum_tensor("m0", [P, 512], F32))
        m1 = ctx.enter_context(nc.psum_tensor("m1", [P, 512], F32))

        w_load, w2_load, x_load = sem("w_load"), sem("w2_load"), [sem(f"x_load{i}") for i in range(8)]
        zero_ready, zero_stored = sem("zero_ready"), sem("zero_stored")
        const_ready = sem("const_ready")
        a_exp, a_ready = sem("a_exp"), sem("a_ready")
        stats_done, mean_done, var_ready, root_ready, xn_ready = (
            sem("stats_done"), sem("mean_done"), sem("var_ready"), sem("root_ready"), sem("xn_ready"))
        head_T, head_Tcopy, head_Tstore = sem("head_T"), sem("head_Tcopy"), [sem("head_Ts0"), sem("head_Ts1")]
        gate_done, wm_full, wm_free = sem("gate_done"), sem("wm_full"), sem("wm_free")
        rt, mask_ready, prefix_ready, gap_ready, gap_exp = (
            sem("rt"), sem("mask_ready"), sem("prefix_ready"), sem("gap_ready"), sem("gap_exp"))
        route_ready, scattered = sem("route_ready"), sem("scattered")
        exp_done, u_done, scan_done, carry_saved = sem("exp_done"), sem("u_done"), sem("scan_done"), sem("carry_saved")
        mul_done, half_done, sum_done = sem("mul_done"), sem("half_done"), sem("sum_done")
        y_skip, gated = sem("y_skip"), sem("gated")
        pj_full, pj_free = sem("pj_full"), sem("pj_free")
        xnT_in, xres_in, mix_out = sem("xnT_in"), sem("xres_in"), sem("mix_out")
        halo_ready, conv_t, conv_done, xin_ready = (
            sem("halo_ready"), sem("conv_t"), sem("conv_done"), sem("xin_ready"))
        pre_ready, sp_min, sp_exp, sp_ln, delta_ready, dx_ready = (
            sem("pre_ready"), sem("sp_min"), sem("sp_exp"), sem("sp_ln"), sem("delta_ready"), sem("dx_ready"))
        bcr_round = sem("bcr_round")
        w1_in = [sem(f"w1_in{i}") for i in range(3)]
        xs_in = [sem(f"xs_in{i}") for i in range(3)]
        ys_out = [sem(f"ys_out{i}") for i in range(3)]
        xsT_full, xsT_ready, h_full, h_act, y_full, y_ready = (
            sem("xsT_full"), sem("xsT_ready"), sem("h_full"), sem("h_act"), sem("y_full"), sem("y_ready"))
        pick_in = [sem(f"pick_in{i}") for i in range(4)]
        mix_in = [sem(f"mix_in{i}") for i in range(4)]
        fin_half, fin_ready = sem("fin_half"), sem("fin_ready")
        fin_out = [sem(f"fin_out{i}") for i in range(4)]

        x_t = x.rearrange("(n p) d -> p n d", p=P)
        mix_t = mix_d.rearrange("(n p) d -> p n d", p=P)
        out_t = out.rearrange("(n p) d -> p n d", p=P)
        rows_t = rows_d.rearrange("(n p) d -> n p d", p=P)
        yrows_t = yrows_d.rearrange("(n p) d -> n p d", p=P)
        N_W = 14
        N_CONST = 6

        block = ctx.enter_context(nc.Block())

        @block.sync
        def _(sp):
            for i in range(8):
                nc.sync.dma_start(xn_all[:, 4 * i:4 * i + 4, :], x_t[:, 4 * i:4 * i + 4, :]).then_inc(x_load[i], 16)
                if i == 0:
                    nc.sync.dma_start(gw[:], gate_w.rearrange("(k p) e -> p k e", p=P)).then_inc(w_load, 16)
            sp.wait_ge(zero_ready, 1)
            zview = rows_d.rearrange("(b p r) d -> b p (r d)", p=P, r=8)
            for b in range(SLOTS // 8):
                nc.sync.dma_start(zview[b], zeros[:]).then_inc(zero_stored, 16)
            with sp.Fori(0, NCH // 2) as i:
                for cc in range(2):
                    sp.wait_ge(head_Tcopy, 2 * i + cc + 1)
                    nc.sync.dma_start(xnT_d[bass.ds(2 * i + cc, 1), :, :].rearrange("o p n -> (o p) n"),
                                      xnT_tmp[:, 2 * cc:2 * cc + 2, :].rearrange("p k t -> p (k t)")
                                      ).then_inc(head_Tstore[cc], 16)
            sp.wait_ge(head_Tstore[0], 16 * NCH // 2)
            sp.wait_ge(head_Tstore[1], 16 * NCH // 2)

            def load_xnT(J):
                nc.sync.dma_start(xnT[:].rearrange("p k t -> p (k t)"),
                                  xnT_d[bass.ds(J, 1), :, :].rearrange("o p n -> (o p) n")).then_inc(xnT_in, 16)

            def expert_of(slot):
                return sp.value_load(slot_e[0:1, bass.ds(slot, 1)], min_val=0, max_val=E - 1)

            def load_w1(e, hf, ring):
                nc.sync.dma_start(w1s[:, ring].rearrange("p k f -> p (k f)"),
                                  w1[bass.ds(2 * e + hf, 1), :, :].rearrange("o p n -> (o p) n")).then_inc(w1_in[ring], 16)

            def load_rows(slot, ring):
                nc.sync.dma_start(xs[:, ring, :], rows_t[bass.ds(slot, 1), :, :].rearrange("o p d -> (o p) d")
                                  ).then_inc(xs_in[ring], 16)

            load_xnT(0)
            sp.wait_ge(route_ready, 1)
            e = expert_of(0)
            load_w1(e, 0, 0)
            load_w1(e, 1, 1)
            load_w1(expert_of(1), 0, 2)
            sp.wait_ge(scattered, 16 * 2 * NT)
            load_rows(0, 0)
            load_rows(1, 1)
            sp.wait_ge(pj_full, pj_ahead(0, PJ_Z + 1) + 1)
            load_xnT(1)

            def body(g, last=False):
                for kk in range(GS):
                    ci, k = kk // STEPS, kk % STEPS
                    J = 2 * g + ci
                    if k == 8 and not last:
                        sp.wait_ge(pj_full, pj_index(J, PJ_Z + 1) + 1)
                        load_xnT(J + 2)
                    if k == 7:
                        if not (isinstance(J, int) and J == 0):
                            sp.wait_ge(pj_free, pj_index(J, PJ_OUT) + 1)
                            nc.sync.dma_start(mix_t[:, bass.ds(TT * (J - 1), TT), :], xres[:]).then_inc(mix_out, 16)
                    if k == 10:
                        wait(sp, mix_out, 16 * J)
                        nc.sync.dma_start(xres[:], x_t[:, bass.ds(TT * J, TT), :]).then_inc(xres_in, 16)
                    for m in range(GM):
                        slot = GM * g + m
                        if kk == BLOCK_AT[m] + 1:
                            if not (last and m == GM - 1):
                                e = expert_of(slot + 1)
                            if not (last and m >= GM - 2):
                                e_next = expert_of(slot + 2)
                            if not (last and m == GM - 1):
                                sp.wait_ge(h_full, 2 * slot + 1)
                                load_w1(e, 1, (2 * m + 3) % 3)
                            if not (last and m >= GM - 2):
                                sp.wait_ge(h_full, 2 * slot + 2)
                                load_w1(e_next, 0, (2 * m + 4) % 3)
                                if not (isinstance(g, int) and g == 0 and m == 0):
                                    sp.wait_ge(ys_out[(m + 2) % 3], 16 * (3 * g + (m + 2) // 3))
                                load_rows(slot + 2, (m + 2) % 3)
                        if kk == BLOCK_AT[m] + 3:
                            sp.wait_ge(y_ready, slot + 1)
                            nc.sync.dma_start(yrows_t[bass.ds(slot, 1), :, :].rearrange("o p d -> (o p) d"),
                                              xs[:, m % 3, :]).then_inc(ys_out[m % 3], 16)

            body(0)
            with sp.Fori(1, GROUPS - 1) as g:
                body(g)
            body(GROUPS - 1, last=True)
            sp.wait_ge(pj_free, pj_index(NCH, PJ_OUT) + 1)
            nc.sync.dma_start(mix_t[:, TT * (NCH - 1):TT * NCH, :], xres[:]).then_inc(mix_out, 16)
            sp.wait_ge(mix_out, 16 * NCH)
            for r in range(3):
                sp.wait_ge(ys_out[r], 16 * SLOTS // 3)

            for n in range(NT + 2):
                if n < NT:
                    b = n % 4
                    wait(sp, fin_out[b], 16 * (n // 4))
                    nc.sync.dma_start(xn_all[:, 3 * b, :], mix_t[:, n, :]).then_inc(mix_in[b], 16)
                if n >= 2:
                    sp.wait_ge(fin_ready, n - 1)
                    nc.sync.dma_start(out_t[:, n - 2, :], xn_all[:, 3 * ((n - 2) % 4), :]).then_inc(fin_out[(n - 2) % 4], 16)
            for b in range(4):
                sp.wait_ge(fin_out[b], 16 * NT // 4)

        @block.gpsimd
        def _(pool):
            nc.gpsimd.memset(zeros[:], 0.0).then_inc(zero_ready, 1)
            nc.gpsimd.memset(ident[:], 0.0)
            nc.gpsimd.memset(half[:, 0, 0:2 * P], 0.0)
            nc.gpsimd.memset(pickf, 0.0).then_inc(const_ready, 1)
            pool.wait_ge(const_ready, 1)
            nc.gpsimd.affine_select(out=ident[:], in_=ident[:], compare_op=ALU.not_equal, fill=1.0, base=0,
                                    pattern=[[-1, P]], channel_multiplier=1)
            nc.gpsimd.affine_select(out=upper, in_=upper, compare_op=ALU.is_ge, fill=1.0, base=0,
                                    pattern=[[-1, P]], channel_multiplier=1)
            nc.gpsimd.memset(ones, 1.0).then_inc(const_ready, 1)
            nc.gpsimd.affine_select(out=pickf, in_=pickf, compare_op=ALU.not_equal, fill=1.0, base=0,
                                    pattern=[[-1, 2 * S]], channel_multiplier=1).then_inc(const_ready, 1)
            pool.wait_ge(const_ready, 3)
            nc.gpsimd.affine_select(out=pickf, in_=pickf, compare_op=ALU.not_equal, fill=1.0, base=-2 * S,
                                    pattern=[[-1, 2 * S]], channel_multiplier=1).then_inc(const_ready, 1)
            nc.gpsimd.iota(em8i, pattern=[[1, E]], base=-E, channel_multiplier=0).then_inc(const_ready, 1)
            nc.gpsimd.iota(sloti, pattern=[[1, SLOTS]], base=0, channel_multiplier=0).then_inc(const_ready, 1)

            pool.wait_ge(route_ready, 1)
            pool.wait_ge(zero_stored, 16 * SLOTS // 8)
            for n in range(NT):
                for c in range(2):
                    nc.gpsimd.indirect_dma_start(
                        out=rows_d, out_offset=bass.IndirectOffsetOnAxis(ap=pos[:, c, n:n + 1], axis=0),
                        in_=xn_all[:, n, :], in_offset=None).then_inc(scattered, 16)

            def make_u(g, kk):
                ci, k = kk // STEPS, kk % STEPS
                J, c, q = 2 * g + ci, k // NQ, k % NQ
                K = GS * g + kk
                if k == 0:
                    pool.wait_ge(dx_ready, J + 1)
                if c == 0:
                    pool.wait_ge(pj_free, spread_use(J, q, 1) + 1)
                wait(pool, scan_done, K - 1)
                nc.gpsimd.tensor_tensor(
                    u[:, kk % 2, :].rearrange("p (s t) -> p s t", s=SQ),
                    dx[:, ci, c, :].unsqueeze(1).broadcast_to([P, SQ, T]),
                    bc[:, 0, SQ * q:SQ * q + SQ, :], ALU.mult).then_inc(u_done, 1)

            def halve(g, kk):
                K = GS * g + kk
                pool.wait_ge(mul_done, K + 1)
                wait(pool, sum_done, K - 1)
                nc.gpsimd.tensor_tensor(half[:, kk % 2, :], prod[:, kk % 2, 0:SQ * T // 2],
                                        prod[:, kk % 2, SQ * T // 2:SQ * T], ALU.add).then_inc(half_done, 1)

            def gate(g, ci, c):
                J = 2 * g + ci
                pool.wait_ge(y_skip, CT * J + c + 1)
                nc.gpsimd.tensor_tensor(gz[:, ci % 2, c, :], xin[:, ci % 2, c, :], gz[:, ci % 2, c, :],
                                        ALU.mult).then_inc(gated, 1)

            def step(g, kk, first, tail):
                if not tail:
                    make_u(g, kk)
                if not (first and kk < 2) and kk - 2 < GS:
                    halve(g, kk - 2)
                if kk % 4 == 3 and not (first and kk == 3):
                    c = (kk // 4 - 1) % CT
                    gate(g, (kk - 7) // STEPS, c)

            for kk in range(GS):
                step(0, kk, True, False)
            with pool.Fori(1, GROUPS) as g:
                for kk in range(GS):
                    step(g, kk, False, False)
            for kk in range(GS, GS + 4):
                step(GROUPS - 1, kk, False, True)

            for r in range(3):
                pool.wait_ge(ys_out[r], 16 * SLOTS // 3)
            for n in range(NT):
                b = n % 4
                if n == 0:
                    pool.wait_ge(sum_done, GS * GROUPS)
                    pool.wait_ge(mul_done, GS * GROUPS)
                wait(pool, fin_ready, n - 3)
                for c in range(2):
                    nc.gpsimd.indirect_dma_start(
                        out=xn_all[:, 3 * b + 1 + c, :], out_offset=None, in_=yrows_d,
                        in_offset=bass.IndirectOffsetOnAxis(ap=pos[:, c, n:n + 1], axis=0)).then_inc(pick_in[b], 16)

        @block.scalar
        def _(act):
            def load(dst, src, s=w_load):
                nc.scalar.dma_start(dst, src).then_inc(s, 16)

            load(xw_tmp, xp_w.rearrange("(c p) j -> p c j", p=P))
            load(dtw_tmp, dt_wT.rearrange("(c p) j -> p c j", p=P))
            load(w_in[:], in_wT.rearrange("(k p) n -> p k n", p=P))
            for r in range(4):
                load(w_bc[:, :, 2 * S * r:2 * S * (r + 1)], bc_wT.rearrange("(c p) j -> p c j", p=P))
            load(w_out[:], out_wT.rearrange("(c p) n -> p c n", p=P))
            load(a_neg[:], A_log.rearrange("(c p) s -> p c s", p=P))
            load(cw[:], conv_w.rearrange("(c p) o k -> p c (o k)", p=P))
            with nc.allow_non_contiguous_dma(reason="three vectors of 512"):
                load(cb[:], conv_b.rearrange("(c p) -> p c", p=P))
                load(dtb[:], dt_b.rearrange("(c p) -> p c", p=P))
                load(dskip[:], D_skip.rearrange("(c p) -> p c", p=P))
            for e in range(E):
                load(w2s[:, e * FT * D:(e + 1) * FT * D], w2[e], w2_load)

            nc.scalar.preload_act_table_set("natural_log_exp_and_others")
            act.wait_ge(w_load, 16 * N_W)
            nc.scalar.activation(a_neg[:], a_neg[:], ACT.Exp).then_inc(a_exp, 1)
            act.wait_ge(var_ready, 1)
            nc.scalar.activation(small[1], small[0], ACT.Sqrt).then_inc(root_ready, 1)

            for jt in range(CT):
                act.wait_ge(wm_full, jt + 1)
                nc.scalar.activation(w_dt[:, jt, :], (m0, m1)[jt % 2][:], ACT.Copy).then_inc(wm_free, 1)

            def copy_T(i, cc, free_ok):
                act.wait_ge(head_T, 2 * i + cc + 1)
                if free_ok:
                    act.wait_ge(head_Tstore[cc], 16 * i)
                nc.scalar.activation(xnT_tmp[:, 2 * cc:2 * cc + 2, :].rearrange("p k t -> p (k t)"),
                                     hs[:, 0, 512 * cc:512 * cc + 512], ACT.Copy).then_inc(head_Tcopy, 1)
            copy_T(0, 0, False)
            copy_T(0, 1, False)
            with act.Fori(1, NCH // 2) as i:
                copy_T(i, 0, True)
                copy_T(i, 1, True)
            act.wait_ge(gap_ready, 1)
            nc.scalar.activation(small[3], small[3], ACT.Exp).then_inc(gap_exp, 1)

            def copy_x(J, pair):
                act.wait_ge(pj_full, pj_ahead(J, PJ_X + pair) + 1)
                if pair == 0:
                    act.wait_ge(halo_ready, J + 1)
                nc.scalar.activation(xraw[:, 2 * pair:2 * pair + 2, TAPS - 1:],
                                     pj[:].rearrange("p (c t) -> p c t", c=2), ACT.Copy).then_inc(pj_free, 1)

            def silus(J, ci):
                for pair in range(2):
                    act.wait_ge(pj_full, pj_ahead(J, PJ_Z + pair) + 1)
                    nc.scalar.activation(gz[:, ci, 2 * pair:2 * pair + 2, :],
                                         pj[:].rearrange("p (c t) -> p c t", c=2), ACT.Silu).then_inc(pj_free, 1)
                for c in range(CT):
                    act.wait_ge(conv_done, CT * J + c + 1)
                    nc.scalar.activation(xin[:, ci, c, :], xc[:, c, :], ACT.Silu,
                                         bias=cb[:, c:c + 1]).then_inc(xin_ready, 1)
                nc.scalar.preload_act_table_set("natural_log_exp_and_others")

            def softplus(J):
                act.wait_ge(sp_min, J + 1)
                nc.scalar.activation(xc[:], xc[:], ACT.Exp).then_inc(sp_exp, 1)
                act.wait_ge(sp_exp, J + 1)
                nc.scalar.activation(xc[:], xc[:], ACT.Ln, bias=1.0).then_inc(sp_ln, 1)

            def spread_copy(J, q, first=False):
                for i in range(4):
                    act.wait_ge(pj_full, spread_use(J, q, i) + 1)
                    if i == 0 and not first:
                        act.wait_ge(u_done, STEPS * (J - 1) + STEPS - NQ + q + 1)
                        act.wait_ge(mul_done, STEPS * (J - 1) + STEPS - NQ + q + 1)
                    s0 = SQ * q + 2 * (i % 2)
                    nc.scalar.activation(bc[:, i // 2, s0:s0 + 2, :].rearrange("p s t -> p (s t)"),
                                         pj[:], ACT.Copy).then_inc(pj_free, 1)

            act.wait_ge(head_Tstore[0], 16 * NCH // 2)
            act.wait_ge(head_Tstore[1], 16 * NCH // 2)
            act.wait_ge(zero_stored, 16 * SLOTS // 8)
            copy_x(0, 0)
            copy_x(0, 1)
            silus(0, 0)
            softplus(0)
            act.wait_ge(scattered, 16 * 2 * NT)
            spread_copy(0, 0, True)
            spread_copy(0, 1, True)
            act.wait_ge(a_ready, 1)

            def body(g, first=False, last=False):
                for kk in range(GS):
                    ci, k = kk // STEPS, kk % STEPS
                    J, c, q = 2 * g + ci, k // NQ, k % NQ
                    K = GS * g + kk
                    if k == 0:
                        act.wait_ge(delta_ready, J + 1)
                    wait(act, mul_done, K - 1)
                    for s in range(SQ):
                        ins = nc.scalar.activation(hs[:, kk % 2, s * T:(s + 1) * T], delta[:, ci, c, :], ACT.Exp,
                                                   scale=a_neg[:, c, SQ * q + s:SQ * q + s + 1])
                    ins.then_inc(exp_done, 1)
                    prep = not (last and ci == 1)
                    if k < 2:
                        spread_copy(J, 2 + k, first and ci == 0)
                    if prep:
                        if k == 2 or k == 3:
                            copy_x(J + 1, k - 2)
                        if k == 7:
                            silus(J + 1, 1 - ci)
                        if k == 10:
                            softplus(J + 1)
                        if k >= 14:
                            spread_copy(J + 1, k - 14)
                    for m in range(GM):
                        if kk == BLOCK_AT[m] + 1:
                            slot = GM * g + m
                            wait(act, y_full, slot)
                            for hf in range(2):
                                act.wait_ge(h_full, 2 * slot + hf + 1)
                                nc.scalar.activation(
                                    hT[:, 4 * hf:4 * hf + 4, :].rearrange("p f n -> p (f n)"),
                                    (m1, m0)[hf][:], ACT.Gelu_apprx_tanh).then_inc(h_act, 1)
                            nc.scalar.preload_act_table_set("natural_log_exp_and_others")

            body(0, first=True)
            with act.Fori(1, GROUPS - 1) as g:
                body(g)
            body(GROUPS - 1, last=True)

        @block.vector
        def _(dve):
            nc.vector.memset(xraw[:, :, 0:TAPS - 1], 0.0).then_inc(halo_ready, 1)
            dve.wait_ge(const_ready, N_CONST)
            nc.vector.tensor_copy(pick[:], pickf)
            nc.vector.tensor_copy(em8, em8i)
            nc.vector.tensor_copy(slotf, sloti)
            dve.wait_ge(a_exp, 1)
            nc.vector.tensor_scalar(a_neg[:], a_neg[:], -1.0, None, ALU.mult).then_inc(a_ready, 1)

            for n in range(NT + 2):
                if n < NT:
                    if n % 4 == 0:
                        dve.wait_ge(x_load[n // 4], 16)
                    nc.vector.bn_stats(stats[:, n, :], xn_all[:, n, :]).then_inc(stats_done, 1)
                if n >= 2:
                    dve.wait_ge(stats_done, n - 1)
                    nc.vector.bn_aggr(mv[:, n - 2, :], stats[:, n - 2, :]).then_inc(mean_done, 1)
            count = [0]

            def then(ins):
                count[0] += 1
                ins.then_inc(rt, 1)
                dve.wait_ge(rt, count[0])

            dve.wait_ge(mean_done, NT)
            nc.vector.tensor_scalar(small[0], mv[:, :, 1], EPS, None, ALU.add).then_inc(var_ready, 1)
            dve.wait_ge(root_ready, 1)
            then(nc.vector.reciprocal(small[2], small[1]))
            then(nc.vector.tensor_tensor(small[3], small[2], small[2], ALU.mult))
            then(nc.vector.tensor_tensor(small[3], small[3], small[0], ALU.mult))
            then(nc.vector.tensor_scalar(small[3], small[3], -0.5, 1.5, ALU.mult, ALU.add))
            then(nc.vector.tensor_tensor(rstd, small[2], small[3], ALU.mult))
            with dve.Fori(0, NT // 4) as i:
                for j in range(4):
                    row = xn_all[:, bass.ds(4 * i + j, 1), :].rearrange("p o d -> p (o d)")
                    nc.vector.tensor_scalar(row, row, mv[:, bass.ds(4 * i + j, 1), 0:1].rearrange("p o k -> p (o k)"),
                                            rstd[:, bass.ds(4 * i + j, 1)], ALU.subtract, ALU.mult
                                            ).then_inc(xn_ready, 1)

            def v(i):
                t = stage if i < 8 else stage2
                return t[:, 256 * (i % 8):256 * (i % 8) + 256].rearrange("p (n e) -> p n e", e=E)

            lg = ysum[:, 0:NT * E].rearrange("p (n e) -> p n e", e=E)
            shape = [P, NT, E]
            em8_b = em8.unsqueeze(1).broadcast_to(shape)
            def over_e(a):
                return a.unsqueeze(2).broadcast_to(shape)

            dve.wait_ge(gate_done, NT)
            best, pick1, second, pick2 = small[0], v(2), small[1], v(4)
            then(nc.vector.tensor_reduce(best, lg, AX_X, ALU.max))
            then(nc.vector.tensor_tensor(v(0), lg, over_e(best), ALU.is_equal))
            then(nc.vector.tensor_tensor(v(1), v(0), em8_b, ALU.mult))
            then(nc.vector.tensor_reduce(small[2], v(1), AX_X, ALU.min))
            then(nc.vector.tensor_tensor(pick1, em8_b, over_e(small[2]), ALU.is_equal))
            then(nc.vector.scalar_tensor_tensor(out=v(3), in0=pick1, scalar=-3.0e38, in1=lg, op0=ALU.mult, op1=ALU.add))
            then(nc.vector.tensor_reduce(second, v(3), AX_X, ALU.max))
            then(nc.vector.tensor_tensor(v(0), v(3), over_e(second), ALU.is_equal))
            then(nc.vector.tensor_tensor(v(1), v(0), em8_b, ALU.mult))
            then(nc.vector.tensor_reduce(small[2], v(1), AX_X, ALU.min))
            then(nc.vector.tensor_tensor(pick2, em8_b, over_e(small[2]), ALU.is_equal))
            nc.vector.tensor_tensor(v(5), pick1, pick2, ALU.add).then_inc(mask_ready, 1)
            nc.vector.tensor_tensor(small[3], second, best, ALU.subtract).then_inc(gap_ready, 1)
            dve.wait_ge(gap_exp, 1)
            then(nc.vector.tensor_scalar(small[4], small[3], 1.0, None, ALU.add))
            then(nc.vector.reciprocal(wgt[:, 0, :], small[4]))
            nc.vector.tensor_tensor(wgt[:, 1, :], small[3], wgt[:, 0, :], ALU.mult)
            dve.wait_ge(prefix_ready, 1)
            below = m0[:, 0:256].rearrange("p (n e) -> p n e", e=E)
            total = m0[:, 256:512].rearrange("p (n e) -> p n e", e=E)
            for e in range(E):
                ins = nc.vector.tensor_tensor_scan(v(6)[:, :, e], ones[:, 0:NT], total[:, :, e], 0.0, ALU.mult, ALU.add)
            then(ins)
            then(nc.vector.tensor_tensor(v(7), v(6), total, ALU.subtract))
            then(nc.vector.tensor_tensor(v(7), v(7), below, ALU.add))
            then(nc.vector.tensor_scalar(e8[0].bitcast(I32), v(6)[:, NT - 1, :], float(P - 1), None, ALU.add))
            then(nc.vector.tensor_scalar(e8[1].bitcast(I32), e8[0].bitcast(I32), 7, None, ALU.arith_shift_right))
            then(nc.vector.tensor_copy(e8[2], e8[1].bitcast(I32)))
            then(nc.vector.tensor_tensor_scan(e8[3], ones[:, 0:E], e8[2], 0.0, ALU.mult, ALU.add))
            then(nc.vector.tensor_tensor(e8[4], e8[3], e8[2], ALU.subtract))
            then(nc.vector.tensor_scalar(e8[5], e8[4], float(P), None, ALU.mult))
            then(nc.vector.tensor_tensor(v(7), v(7), e8[5].unsqueeze(1).broadcast_to(shape), ALU.add))
            for c, one in ((0, pick1), (1, pick2)):
                then(nc.vector.tensor_tensor(v(0), one, v(7), ALU.mult))
                then(nc.vector.tensor_reduce(small[2], v(0), AX_X, ALU.add))
                then(nc.vector.tensor_copy(pos[:, c, :], small[2]))
            ends = stage2[:, 0:SLOTS * E].rearrange("p (n e) -> p n e", e=E)
            then(nc.vector.tensor_tensor(ends, slotf.unsqueeze(2).broadcast_to([P, SLOTS, E]),
                                         e8[3].unsqueeze(1).broadcast_to([P, SLOTS, E]), ALU.is_ge))
            then(nc.vector.tensor_reduce(stage2[:, 1024:1024 + SLOTS], ends, AX_X, ALU.add))
            nc.vector.tensor_scalar(slot_e[:], stage2[:, 1024:1024 + SLOTS], float(E - 1), None, ALU.min
                                    ).then_inc(route_ready, 1)

            def conv(J, pair):
                dve.wait_ge(pj_free, pj_ahead(J, PJ_X + pair) + 1)
                if pair == 0:
                    wait(dve, xin_ready, CT * J)
                for tap in range(TAPS):
                    for j in range(2):
                        c = 2 * pair + j
                        src = xraw[:, c, tap:tap + T]
                        if tap == 0:
                            nc.vector.tensor_scalar(xc[:, c, :], src, cw[:, c, 0:1], None, ALU.mult).then_inc(conv_t, 1)
                            continue
                        dve.wait_ge(conv_t, 12 * J + 6 * pair + 2 * tap + j - 1)
                        ins = nc.vector.scalar_tensor_tensor(out=xc[:, c, :], in0=src, scalar=cw[:, c, tap:tap + 1],
                                                             in1=xc[:, c, :], op0=ALU.mult, op1=ALU.add)
                        ins.then_inc(conv_done if tap == TAPS - 1 else conv_t, 1)
                if pair == 1:
                    nc.vector.tensor_copy(xraw[:, :, 0:TAPS - 1], xraw[:, :, T:T + TAPS - 1]).then_inc(halo_ready, 1)

            def copy_delta(J, ci, pair):
                dve.wait_ge(pj_full, pj_ahead(J, PJ_DT + pair) + 1)
                for j in range(2):
                    c = 2 * pair + j
                    ins = nc.vector.tensor_scalar(delta[:, ci, c, :], pj[:, T * j:T * j + T], dtb[:, c:c + 1], None,
                                                  ALU.add)
                ins.then_inc(pj_free, 1)

            def cut(J, ci):
                dve.wait_ge(pj_free, pj_ahead(J, PJ_DT + 1) + 1)
                nc.vector.tensor_scalar(xc[:], delta[:, ci], SP_CUT, None, ALU.min).then_inc(sp_min, 1)

            def split_bc(J):
                dve.wait_ge(pj_full, pj_ahead(J, PJ_BC) + 1)
                nc.vector.tensor_copy(bcr[:], pj[:, 0:T]).then_inc(bcr_round, 1)
                dve.wait_ge(bcr_round, J + 1)
                ins = nc.vector.tensor_tensor(bcr[2 * S:4 * S, :], pj[2 * S:4 * S, 0:T],
                                              bcr[2 * S:4 * S, :].bitcast(F32), ALU.subtract)
                ins.then_inc(pj_free, 1)

            def finish_delta(J, ci):
                dve.wait_ge(sp_ln, J + 1)
                nc.vector.tensor_tensor(delta[:, ci], delta[:, ci], xc[:], ALU.max).then_inc(delta_ready, 1)
                dve.wait_ge(delta_ready, J + 1)
                nc.vector.tensor_tensor(dx[:, ci], delta[:, ci], xin[:, ci], ALU.mult).then_inc(dx_ready, 1)

            def skip_term(g, ci, c):
                J = 2 * g + ci
                dve.wait_ge(sum_done, STEPS * J + NQ * c + NQ)
                nc.vector.scalar_tensor_tensor(out=xin[:, ci % 2, c, :], in0=xin[:, ci % 2, c, :], scalar=dskip[:, c:c + 1],
                                               in1=ysum[:, 0:T], op0=ALU.mult, op1=ALU.add).then_inc(y_skip, 1)

            def add_x(J):
                dve.wait_ge(pj_full, pj_index(J + 1, PJ_OUT) + 1)
                dve.wait_ge(xres_in, 16 * (J + 1))
                ins = nc.vector.tensor_tensor(xres[:].rearrange("p n d -> p (n d)"), pj[:],
                                              xres[:].rearrange("p n d -> p (n d)"), ALU.add)
                ins.then_inc(pj_free, 1)

            conv(0, 0)
            conv(0, 1)
            copy_delta(0, 0, 0)
            copy_delta(0, 0, 1)
            cut(0, 0)
            split_bc(0)
            finish_delta(0, 0)

            def body(g, first=False, last=False):
                for kk in range(GS):
                    ci, k = kk // STEPS, kk % STEPS
                    J, c, q = 2 * g + ci, k // NQ, k % NQ
                    K = GS * g + kk
                    prep = not (last and ci == 1)
                    dve.wait_ge(exp_done, K + 1)
                    dve.wait_ge(u_done, K + 1)
                    at_zero = first and ci == 0
                    if not at_zero:
                        dve.wait_ge(carry_saved, K - STEPS + 1)
                    for s in range(SQ):
                        h = hs[:, kk % 2, s * T:(s + 1) * T]
                        start = 0.0 if at_zero else carry[:, c, SQ * q + s:SQ * q + s + 1]
                        ins = nc.vector.tensor_tensor_scan(h, h, u[:, kk % 2, s * T:(s + 1) * T], start, ALU.mult, ALU.add)
                    ins.then_inc(scan_done, 1)

                    if k % 4 == 3 and not (first and kk == 3):
                        skip_term(g, (kk - 7) // STEPS, (kk // 4 - 1) % CT)
                    if k == 6 and not at_zero:
                        add_x(J - 1)
                    if prep:
                        if k == 4 or k == 5:
                            conv(J + 1, k - 4)
                        if k == 8 or k == 9:
                            copy_delta(J + 1, 1 - ci, k - 8)
                        if k == 9:
                            cut(J + 1, 1 - ci)
                            split_bc(J + 1)
                        if k == 11:
                            finish_delta(J + 1, 1 - ci)
                    for m in range(GM):
                        slot = GM * g + m
                        if kk == BLOCK_AT[m]:
                            dve.wait_ge(xsT_full, slot + 1)
                            wait(dve, h_full, 2 * slot)
                            nc.vector.tensor_copy(xsT[:].rearrange("p k n -> p (k n)"), m0[:, 0:KD * P]
                                                  ).then_inc(xsT_ready, 1)
                        if kk == BLOCK_AT[m] + 3:
                            dve.wait_ge(y_full, slot + 1)
                            nc.vector.tensor_copy(xs[:, m % 3, :], m1[:, 0:D]).then_inc(y_ready, 1)

                    dve.wait_ge(scan_done, K + 1)
                    nc.vector.tensor_copy(carry[:, c, SQ * q:SQ * q + SQ],
                                          hs[:, kk % 2, :].rearrange("p (s t) -> p s t", s=SQ)[:, :, T - 1]
                                          ).then_inc(carry_saved, 1)
                    if c == 0:
                        dve.wait_ge(pj_free, spread_use(J, q, 3) + 1)
                    wait(dve, half_done, K - 1)
                    nc.vector.tensor_tensor(prod[:, kk % 2, :], hs[:, kk % 2, :],
                                            bc[:, 1, SQ * q:SQ * q + SQ, :].rearrange("p s t -> p (s t)"),
                                            ALU.mult).then_inc(mul_done, 1)

            body(0, first=True)
            with dve.Fori(1, GROUPS - 1) as g:
                body(g)
            body(GROUPS - 1, last=True)
            skip_term(GROUPS - 1, 1, CT - 1)
            add_x(NCH - 1)

            for n in range(NT):
                b = n % 4
                acc = xn_all[:, 3 * b, :]
                dve.wait_ge(mix_in[b], 16 * (n // 4 + 1))
                dve.wait_ge(pick_in[b], 32 * (n // 4 + 1))
                nc.vector.scalar_tensor_tensor(out=acc, in0=xn_all[:, 3 * b + 1, :], scalar=wgt[:, 0, n:n + 1], in1=acc,
                                               op0=ALU.mult, op1=ALU.add).then_inc(fin_half, 1)
                dve.wait_ge(fin_half, n + 1)
                nc.vector.scalar_tensor_tensor(out=acc, in0=xn_all[:, 3 * b + 2, :], scalar=wgt[:, 1, n:n + 1], in1=acc,
                                               op0=ALU.mult, op1=ALU.add).then_inc(fin_ready, 1)

        @block.tensor
        def _(pe):
            pe.wait_ge(w_load, 16 * N_W)
            for jt in range(CT):
                wait(pe, wm_free, jt - 1)
                for it in range(CT):
                    ins = nc.tensor.matmul((m0, m1)[jt % 2][:], xw_tmp[:, it, P * jt:P * jt + P], dtw_tmp[:, it, :],
                                           start=(it == 0), stop=(it == CT - 1))
                ins.then_inc(wm_full, 1)
            pe.wait_ge(const_ready, N_CONST)

            def head(i, free_ok):
                for cc in range(2):
                    bank = hs[:, 0, 512 * cc:512 * cc + 512]
                    if free_ok:
                        pe.wait_ge(head_Tcopy, 2 * i + cc - 1)
                    for tt in range(TT):
                        pe.wait_ge(xn_ready, 4 * i + 2 * cc + tt + 1)
                        for kd in range(KD):
                            ins = nc.tensor.transpose(bank[:, kd * T + tt * P:kd * T + tt * P + P],
                                                      xn_all[:, 4 * i + 2 * cc + tt, kd * P:kd * P + P], ident[:])
                    ins.then_inc(head_T, 1)
                for cc in range(2):
                    pe.wait_ge(head_Tcopy, 2 * i + cc + 1)
                    for tt in range(TT):
                        for kd in range(KD):
                            ins = nc.tensor.matmul(ysum[:, bass.ds(E * (4 * i + 2 * cc + tt), E)],
                                                   xnT_tmp[:, 2 * cc + kd, tt * P:tt * P + P], gw[:, kd, :],
                                                   start=(kd == 0), stop=(kd == KD - 1))
                        ins.then_inc(gate_done, 1)

            for i in range(NT // 4):
                head(i, i > 0)
            pe.wait_ge(mask_ready, 1)
            mask = stage[:, 5 * 256:6 * 256]
            nc.tensor.matmul(m0[:, 0:256], upper, mask, start=True, stop=True)
            nc.tensor.matmul(m0[:, 256:512], ones, mask, start=True, stop=True).then_inc(prefix_ready, 1)

            def in_proj(J, r, m):
                n = pj_ahead(J, r)
                wait(pe, pj_free, n)
                if m == 0:
                    pe.wait_ge(xnT_in, 16 * (J + 1))
                for j in range(2):
                    for kd in range(KD):
                        ins = nc.tensor.matmul(pj[:, T * j:T * j + T], w_in[:, kd, P * (m + j):P * (m + j + 1)],
                                               xnT[:, kd, :], start=(kd == 0), stop=(kd == KD - 1))
                ins.then_inc(pj_full, 1)

            def delta_proj(J, ci, pair):
                wait(pe, pj_free, pj_ahead(J, PJ_DT + pair))
                if pair == 0:
                    pe.wait_ge(xin_ready, CT * (J + 1))
                for j in range(2):
                    e0 = P * (2 * pair + j)
                    for c in range(CT):
                        ins = nc.tensor.matmul(pj[:, T * j:T * j + T], w_dt[:, c, e0:e0 + P], xin[:, ci, c, :],
                                               start=(c == 0), stop=(c == CT - 1))
                ins.then_inc(pj_full, 1)

            def bc_proj(J, ci):
                wait(pe, pj_free, pj_ahead(J, PJ_BC))
                for c in range(CT):
                    ins = nc.tensor.matmul(pj[:, 0:T], w_bc[:, c, :], xin[:, ci, c, :],
                                           start=(c == 0), stop=(c == CT - 1))
                ins.then_inc(pj_full, 1)

            def spread(J, q, i):
                wait(pe, pj_free, spread_use(J, q, i))
                for j in range(2):
                    row = S * (i // 2) + SQ * q + 2 * (i % 2) + j
                    ins = nc.tensor.matmul(pj[:, T * j:T * j + T], pick[:, row:row + 1].broadcast_to([P, P]), bcr[:],
                                           start=True, stop=True)
                ins.then_inc(pj_full, 1)

            def out_proj(J, ci):
                wait(pe, pj_free, pj_index(J + 1, PJ_OUT))
                pe.wait_ge(gated, CT * (J + 1))
                for tt in range(TT):
                    for c in range(CT):
                        ins = nc.tensor.matmul(pj[:, D * tt:D * tt + D], gz[:, ci, c, P * tt:P * tt + P], w_out[:, c, :],
                                               start=(c == 0), stop=(c == CT - 1))
                ins.then_inc(pj_full, 1)

            def sum_states(g, kk):
                K = GS * g + kk
                k = kk % STEPS
                q = k % NQ
                pe.wait_ge(half_done, K + 1)
                if q == 0:
                    if isinstance(K, int):
                        wait(pe, y_skip, K // NQ)
                    else:
                        pe.wait_ge(y_skip, CT * 2 * g + kk // NQ)
                for j in range(2):
                    ins = nc.tensor.matmul(ysum[:, 0:T], ident[:], half[:, kk % 2, T * j:T * j + T],
                                           start=(q == 0 and j == 0), stop=(q == NQ - 1 and j == 1))
                ins.then_inc(sum_done, 1)

            def block_T(g, m):
                slot = GM * g + m
                pe.wait_ge(xs_in[m % 3], 16 * (3 * g + m // 3 + 1))
                wait(pe, h_act, 2 * slot)
                for kd in range(KD):
                    ins = nc.tensor.transpose(m0[:, P * kd:P * kd + P], xs[:, m % 3, P * kd:P * kd + P], ident[:])
                ins.then_inc(xsT_full, 1)

            def block_h(g, m, hf):
                slot = GM * g + m
                if hf == 0:
                    wait(pe, y_ready, slot)
                    pe.wait_ge(xsT_ready, slot + 1)
                hi = 2 * m + hf
                pe.wait_ge(w1_in[hi % 3], 16 * (6 * g + hi // 3 + 1))
                for f in range(4):
                    for kd in range(KD):
                        ins = nc.tensor.matmul((m1, m0)[hf][:, P * f:P * f + P], w1s[:, hi % 3, kd, P * f:P * f + P],
                                               xsT[:, kd, :], start=(kd == 0), stop=(kd == KD - 1))
                ins.then_inc(h_full, 1)

            def block_y(g, m):
                slot = GM * g + m
                e = pe.value_load(slot_e[0:1, bass.ds(slot, 1)], min_val=0, max_val=E - 1)
                pe.wait_ge(h_act, 2 * slot + 2)
                for f in range(FT):
                    ins = nc.tensor.matmul(m1[:, 0:D], hT[:, f, :], w2s[:, bass.ds(e * (FT * D) + f * D, D)],
                                           start=(f == 0), stop=(f == FT - 1))
                ins.then_inc(y_full, 1)

            in_proj(0, PJ_X, 0)
            in_proj(0, PJ_X + 1, 2)
            in_proj(0, PJ_Z, 4)
            in_proj(0, PJ_Z + 1, 6)
            delta_proj(0, 0, 0)
            delta_proj(0, 0, 1)
            bc_proj(0, 0)
            for q in range(2):
                for i in range(4):
                    if q == 0 and i == 0:
                        pe.wait_ge(pj_free, pj_ahead(0, PJ_BC) + 1)
                    spread(0, q, i)
            pe.wait_ge(w2_load, 16 * E)
            pe.wait_ge(route_ready, 1)

            def body(g, first=False, last=False):
                for kk in range(GS):
                    ci, k = kk // STEPS, kk % STEPS
                    J = 2 * g + ci
                    prep = not (last and ci == 1)
                    for m in range(GM):
                        if kk == BLOCK_AT[m] + 3:
                            block_y(g, m)
                    for m in range(GM):
                        if kk == BLOCK_AT[m]:
                            block_T(g, m)
                    if k < 2:
                        for i in range(4):
                            spread(J, 2 + k, i)
                    if prep and (k == 2 or k == 3):
                        in_proj(J + 1, PJ_X + k - 2, 2 * (k - 2))
                    if k == 6 and not (first and ci == 0):
                        out_proj(J - 1, 1 - ci)
                    if prep:
                        if k == 7:
                            in_proj(J + 1, PJ_Z, 4)
                            in_proj(J + 1, PJ_Z + 1, 6)
                        if k == 8:
                            delta_proj(J + 1, 1 - ci, 0)
                        if k == 9:
                            delta_proj(J + 1, 1 - ci, 1)
                            bc_proj(J + 1, 1 - ci)
                        if k >= 14:
                            for i in range(4):
                                spread(J + 1, k - 14, i)
                    for m in range(GM):
                        if kk == BLOCK_AT[m] + 1:
                            block_h(g, m, 0)
                            block_h(g, m, 1)
                    if not (first and kk < 3):
                        sum_states(g, kk - 3)

            body(0, first=True)
            with pe.Fori(1, GROUPS - 1) as g:
                body(g)
            body(GROUPS - 1, last=True)
            for kk in range(GS - 3, GS):
                sum_states(GROUPS - 1, kk)
            out_proj(NCH - 1, 1)


_INS = {
    "x": (L, D), "in_wT": (D, 2 * DI), "conv_w": (DI, 1, TAPS), "conv_b": (DI,), "xp_w": (DI, DI),
    "bc_wT": (DI, 2 * S), "dt_wT": (DI, DI), "dt_b": (DI,), "A_log": (DI, S), "D_skip": (DI,),
    "out_wT": (DI, D), "gate_w": (D, E), "w1": (2 * E, P, KD * HF), "w2": (E, P, FT * D),
}


def kernel(L0_attn_x, L0_attn_in_proj_w, L0_attn_conv_w, L0_attn_conv_b, L0_attn_x_proj_w, L0_attn_dt_proj_w,
           L0_attn_dt_proj_b, L0_attn_A_log, L0_attn_D, L0_attn_out_proj_w, L0_ffn_gate_w, L0_ffn_w1, L0_ffn_w2):
    import concourse.bacc as bacc
    from concourse.bass_utils import run_bass_kernel_spmd

    w1 = np.asarray(L0_ffn_w1).reshape(E, KD, P, 2, HF).transpose(0, 3, 2, 1, 4).reshape(2 * E, P, KD * HF)
    w2 = np.asarray(L0_ffn_w2).reshape(E, FT, P, D).transpose(0, 2, 1, 3).reshape(E, P, FT * D)
    xp = np.asarray(L0_attn_x_proj_w)
    arrays = {
        "x": np.asarray(L0_attn_x).reshape(L, D), "in_wT": np.asarray(L0_attn_in_proj_w).T,
        "conv_w": L0_attn_conv_w, "conv_b": L0_attn_conv_b, "xp_w": xp[:DI], "bc_wT": xp[DI:].T,
        "dt_wT": np.asarray(L0_attn_dt_proj_w).T, "dt_b": L0_attn_dt_proj_b, "A_log": L0_attn_A_log,
        "D_skip": L0_attn_D, "out_wT": np.asarray(L0_attn_out_proj_w).T, "gate_w": L0_ffn_gate_w, "w1": w1, "w2": w2,
    }
    arrays = {k: np.ascontiguousarray(a) for k, a in arrays.items()}
    nc = bacc.Bacc("TRN2", target_bir_lowering=False, num_devices=1)
    aps = [nc.dram_tensor(k, shape, F32, kind="ExternalInput").ap() for k, shape in _INS.items()]
    out = nc.dram_tensor("out", (L, D), F32, kind="ExternalOutput").ap()
    mamba_moe_kernel(nc, *aps, out)
    r = run_bass_kernel_spmd(nc, [arrays], core_ids=[0])
    return r.results[0]["out"].reshape(1, L, D)
```

```python
from contextlib import ExitStack

import numpy as np

import concourse.bass as bass
from concourse import mybir

ALU = mybir.AluOpType
ACT = mybir.ActivationFunctionType
F32 = mybir.dt.float32
F32R = mybir.dt.float32r
I32 = mybir.dt.int32
AX_X = mybir.AxisListType.X

P = 128
L = 4096
D = 256
KD = D // P
DI = 512
CT = DI // P
S = 16
TAPS = 4
T = 256
NCH = L // T
TT = T // P
NT = L // P
SQ = 4
NQ = S // SQ
STEPS = CT * NQ
E = 8
F = 1024
FT = F // P
HF = F // 2
SLOTS = 72
GROUPS = NCH // 2
GS = 2 * STEPS
GM = SLOTS // (GROUPS - 2)
BLOCK_AT = [m * GS // GM for m in range(GM - 1)] + [GS - 4]
FOLD_FROM = GS - 4
AHEAD = 2
EPS = 1e-5
SP_CUT = 30.0

PJ_X, PJ_OUT, PJ_Z, PJ_DT, PJ_BC, PJ_SPREAD = 8, 10, 11, 13, 15, 16
PJ_HEAD = 15


def pj_index(J, r):
    if isinstance(J, int) and J == 0 and r < PJ_OUT:
        return PJ_HEAD + r
    if isinstance(J, int) and J >= NCH - 1 and r == PJ_OUT:
        return PJ_HEAD - 1 + 24 * (NCH - 1) + PJ_X + J - (NCH - 1)
    return PJ_HEAD - 1 + 24 * J + r


def pj_ahead(J, r):
    if isinstance(J, int) and J == 0:
        return {PJ_X: 0, PJ_X + 1: 1, PJ_Z: 2, PJ_Z + 1: 3, PJ_DT: 4, PJ_DT + 1: 5, PJ_BC: 6}.get(r, r - PJ_SPREAD + 7)
    return pj_index(J - 1, r)


def spread_use(J, q, i):
    if q < 2:
        return pj_ahead(J, PJ_SPREAD + 4 * q + i)
    return pj_index(J, 4 * (q - 2) + i)




def wait(eng, sem, value):
    if isinstance(value, int) and value <= 0:
        return
    eng.wait_ge(sem, value)


def mamba_moe_kernel(nc, x, in_wT, conv_w, conv_b, xp_w, bc_wT, dt_wT, dt_b, A_log, D_skip, out_wT,
                     gate_w, w1, w2, out):
    with ExitStack() as ctx:
        def sb(name, shape, dt=F32):
            return ctx.enter_context(nc.sbuf_tensor(name, shape, dt))

        def sem(name):
            return ctx.enter_context(nc.semaphore(name))

        xnT_d = nc.dram_tensor("xnT_d", [NCH, P, KD * T], F32, kind="Internal").ap()
        rows_d = nc.dram_tensor("rows_d", [(SLOTS + 8) * P, D], F32, kind="Internal").ap()
        yrows_d = nc.dram_tensor("yrows_d", [SLOTS * P, D], F32, kind="Internal").ap()
        mix_d = nc.dram_tensor("mix_d", [L, D], F32, kind="Internal").ap()

        w2s = sb("w2s", [P, E * FT * D])
        w1s = sb("w1s", [P, 3, KD, HF])
        w_in = sb("w_in", [P, KD, 2 * DI])
        w_dt = sb("w_dt", [P, CT, DI])
        w_bc = sb("w_bc", [P, CT, P])
        w_out = sb("w_out", [P, CT, D])
        ident = sb("ident", [P, P])
        pick = sb("pick", [P, 2 * S], F32R)
        a_neg = sb("a_neg", [P, CT, S])
        cw = sb("cw", [P, CT, TAPS])
        cb = sb("cb", [P, CT])
        dtb = sb("dtb", [P, CT])
        dskip = sb("dskip", [P, CT])
        gw = sb("gw", [P, KD, E])

        bc = sb("bc", [P, 2, S, T])
        xnT = sb("xnT", [P, KD, T])
        xres = sb("xres", [P, TT, D])
        xraw = sb("xraw", [P, CT, TAPS - 1 + T])
        xin = sb("xin", [P, 2, CT, T])
        delta = sb("delta", [P, 2, CT, T])
        dx = sb("dx", [P, 2, CT, T])
        gz = sb("gz", [P, 2, CT, T])
        u = sb("u", [P, 2, SQ * T])
        prod = sb("prod", [P, 2, SQ * T])
        half = sb("half", [P, 4, SQ * T // 2])
        carry = sb("carry", [P, CT, S])
        bcr = sb("bcr", [P, T], F32R)

        xs = sb("xs", [P, 3, D])
        xsT = sb("xsT", [P, KD, P])
        hT = sb("hT", [P, FT, P])

        pos = sb("pos", [P, 2, NT], I32)
        wgt = sb("wgt", [P, 2, NT])
        slot_e = sb("slot_e", [P, SLOTS + AHEAD], I32)

        xc = dx
        xnT_all = w2s[:, 0:L * KD].rearrange("p (j k t) -> p j k t", k=KD, t=T)
        xn_all = w2s[:, L * KD:].rearrange("p (n d) -> p n d", d=D)
        xw_tmp = delta.rearrange("p a c t -> p (a c t)").rearrange("p (c j) -> p c j", c=CT)
        dtw_tmp = dx.rearrange("p a c t -> p (a c t)").rearrange("p (c j) -> p c j", c=CT)
        w1s_flat = w1s.rearrange("p r k f -> p (r k f)")
        hT_flat = hT.rearrange("p f n -> p (f n)")
        zeros = w1s_flat[:, 0:8 * D]
        stats = w1s_flat[:, 8 * D:8 * D + 6 * NT].rearrange("p (n k) -> p n k", k=6)
        mv = w1s_flat[:, 9 * D:9 * D + 2 * NT].rearrange("p (n k) -> p n k", k=2)
        rstd = w1s_flat[:, 10 * D:10 * D + NT]
        ends_sum = w1s_flat[:, 11 * D:11 * D + SLOTS]
        fin = w1s_flat.rearrange("p (b d) -> p b d", d=D)
        upper = half[:, 0, 0:P]
        ones = half[:, 0, P:2 * P]
        pickf = half[:, 1, 64:96]
        em8i = half[:, 1, 96:104].bitcast(I32)
        em8 = half[:, 1, 104:112]
        sloti = half[:, 1, 112:112 + SLOTS].bitcast(I32)
        slotf = half[:, 1, 192:192 + SLOTS]
        small = [half[:, 1, 272 + 32 * i:304 + 32 * i] for i in range(6)]
        e8 = [half[:, 1, 464 + 8 * i:472 + 8 * i] for i in range(6)]

        hs = ctx.enter_context(nc.psum_tensor("hs", [P, 2, SQ * T], F32))
        ysum = ctx.enter_context(nc.psum_tensor("ysum", [P, 512], F32))
        pj = ctx.enter_context(nc.psum_tensor("pj", [P, 512], F32))
        m0 = ctx.enter_context(nc.psum_tensor("m0", [P, 512], F32))
        m1 = ctx.enter_context(nc.psum_tensor("m1", [P, 512], F32))

        def hs_bank(J):
            return hs[:, J // 2 % 2, 512 * (J % 2):512 * (J % 2) + 512]

        w_first, w_load, w2_load, x_load = sem("w_first"), sem("w_load"), sem("w2_load"), [sem(f"x_load{i}") for i in range(8)]
        zero_ready, zero_stored = sem("zero_ready"), sem("zero_stored")
        const_ready, pick_ready = sem("const_ready"), sem("pick_ready")
        a_exp, a_ready = sem("a_exp"), sem("a_ready")
        stats_done, mean_done, var_ready, root_ready, xn_ready = (
            sem("stats_done"), sem("mean_done"), sem("var_ready"), sem("root_ready"), sem("xn_ready"))
        head_T, head_Tcopy, head_Tstore = sem("head_T"), sem("head_Tcopy"), sem("head_Tstore")
        gate_done, wm_full, wm_free = sem("gate_done"), sem("wm_full"), sem("wm_free")
        rt, mask_ready, prefix_ready, gap_ready, gap_exp = (
            sem("rt"), sem("mask_ready"), sem("prefix_ready"), sem("gap_ready"), sem("gap_exp"))
        route_ready, scattered = sem("route_ready"), sem("scattered")
        exp_done, u_done, scan_done, carry_saved = sem("exp_done"), sem("u_done"), sem("scan_done"), sem("carry_saved")
        mul_done, half_done, sum_done = sem("mul_done"), sem("half_done"), sem("sum_done")
        y_skip, gated = sem("y_skip"), sem("gated")
        pj_full, pj_free = sem("pj_full"), sem("pj_free")
        xnT_in, xres_in, mix_out = sem("xnT_in"), sem("xres_in"), sem("mix_out")
        halo_ready, conv_t, conv_done, xin_ready = (
            sem("halo_ready"), sem("conv_t"), sem("conv_done"), sem("xin_ready"))
        pre_ready, sp_min, sp_exp, sp_ln, delta_ready, dx_ready = (
            sem("pre_ready"), sem("sp_min"), sem("sp_exp"), sem("sp_ln"), sem("delta_ready"), sem("dx_ready"))
        bcr_round, z_ready = sem("bcr_round"), sem("z_ready")
        w1_in = [sem(f"w1_in{i}") for i in range(3)]
        xs_in = [sem(f"xs_in{i}") for i in range(3)]
        ys_out = [sem(f"ys_out{i}") for i in range(3)]
        xsT_full, xsT_ready, h_full, h_act, y_full, y_ready = (
            sem("xsT_full"), sem("xsT_ready"), sem("h_full"), sem("h_act"), sem("y_full"), sem("y_ready"))
        pick_in = [sem(f"pick_in{i}") for i in range(4)]
        mix_in = [sem(f"mix_in{i}") for i in range(4)]
        fin_half, fin_ready = sem("fin_half"), sem("fin_ready")
        fin_out = [sem(f"fin_out{i}") for i in range(4)]

        x_t = x.rearrange("(n p) d -> p n d", p=P)
        mix_t = mix_d.rearrange("(n p) d -> p n d", p=P)
        out_t = out.rearrange("(n p) d -> p n d", p=P)
        rows_t = rows_d.rearrange("(n p) d -> n p d", p=P)
        yrows_t = yrows_d.rearrange("(n p) d -> n p d", p=P)
        N_W = 12
        N_CONST = 6

        block = ctx.enter_context(nc.Block())

        @block.sync
        def _(sp):
            for i in range(8):
                nc.sync.dma_start(xn_all[:, 4 * i:4 * i + 4, :], x_t[:, 4 * i:4 * i + 4, :]).then_inc(x_load[i], 16)
            sp.wait_ge(w_load, 16 * N_W)
            for J in range(NCH):
                sp.wait_ge(head_Tcopy, J + 1)
                nc.sync.dma_start(xnT_d[J], xnT_all[:, J].rearrange("p k t -> p (k t)")).then_inc(head_Tstore, 16)
            sp.wait_ge(zero_ready, 1)
            zview = rows_d.rearrange("(b p r) d -> b p (r d)", p=P, r=8)
            for b in range(SLOTS // 8 + 1):
                nc.sync.dma_start(zview[b], zeros).then_inc(zero_stored, 16)
            sp.wait_ge(head_Tstore, 16 * NCH)

            def load_xnT(J):
                nc.sync.dma_start(xnT[:].rearrange("p k t -> p (k t)"),
                                  xnT_d[bass.ds(J, 1), :, :].rearrange("o p n -> (o p) n")).then_inc(xnT_in, 16)

            def expert_of(slot):
                return sp.value_load(slot_e[0:1, bass.ds(slot, 1)], min_val=0, max_val=E - 1)

            def load_w1(e, hf, ring):
                nc.sync.dma_start(w1s[:, ring].rearrange("p k f -> p (k f)"),
                                  w1[bass.ds(2 * e + hf, 1), :, :].rearrange("o p n -> (o p) n")).then_inc(w1_in[ring], 16)

            def load_rows(slot, ring):
                nc.sync.dma_start(xs[:, ring, :], rows_t[bass.ds(slot, 1), :, :].rearrange("o p d -> (o p) d")
                                  ).then_inc(xs_in[ring], 16)

            def load_w2(e):
                nc.sync.dma_start(w2s[:, e * FT * D:(e + 1) * FT * D], w2[e]).then_inc(w2_load, 16)

            def load_mix(n):
                b = n % 4
                sp.wait_ge(mix_out, 16 * (n // TT + 1))
                if n == 0:
                    for r in range(3):
                        sp.wait_ge(w1_in[r], 16 * (2 * SLOTS // 3 + 1))
                    sp.wait_ge(h_full, 2 * SLOTS + 2)
                wait(sp, fin_out[b], 16 * (n // 4))
                nc.sync.dma_start(fin[:, 3 * b, :], mix_t[:, n, :]).then_inc(mix_in[b], 16)

            def store_out(n):
                sp.wait_ge(fin_ready, n + 1)
                nc.sync.dma_start(out_t[:, n, :], fin[:, 3 * (n % 4), :]).then_inc(fin_out[n % 4], 16)

            load_xnT(1)
            sp.wait_ge(gate_done, NT)
            for e in range(E // 2):
                load_w2(e)

            def body(g, first=False, last=False):
                blocks = not (first or last)
                for kk in range(GS):
                    ci, k = kk // STEPS, kk % STEPS
                    J = 2 * g + ci
                    if k == 8 and not last:
                        sp.wait_ge(pj_full, pj_index(J, PJ_Z + 1) + 1)
                        load_xnT(J + 2)
                    if k == 7:
                        if not (first and ci == 0):
                            sp.wait_ge(pj_free, pj_index(J, PJ_OUT) + 1)
                            nc.sync.dma_start(mix_t[:, bass.ds(TT * (J - 1), TT), :], xres[:]).then_inc(mix_out, 16)
                    if k == 10:
                        wait(sp, mix_out, 16 * J)
                        nc.sync.dma_start(xres[:], x_t[:, bass.ds(TT * J, TT), :]).then_inc(xres_in, 16)
                    if blocks:
                        for m in range(GM):
                            block_loads(g, kk, m)
                        for m in range(GM):
                            store_block(g, kk, m)
                        for m in range(GM):
                            block_rows(g, kk, m)
                    if last:
                        if kk >= 4:
                            store_out(kk - 4)
                        if kk < NT - TT:
                            load_mix(kk)

            def block_loads(g, kk, m):
                slot = GM * (g - 1) + m
                if kk == BLOCK_AT[m] + 1:
                    e, e_next = expert_of(slot + 1), expert_of(slot + 2)
                    sp.wait_ge(h_full, 2 * slot + 3)
                    load_w1(e, 1, (2 * m + 3) % 3)
                    sp.wait_ge(h_full, 2 * slot + 4)
                    load_w1(e_next, 0, (2 * m + 4) % 3)

            def block_rows(g, kk, m):
                slot = GM * (g - 1) + m
                if kk == BLOCK_AT[m] + 1:
                    sp.wait_ge(ys_out[(m + 2) % 3], 16 * (4 * (g - 1) + (m + 2) // 3 + 1))
                    load_rows(slot + 2, (m + 2) % 3)

            def store_block(g, kk, m):
                slot = GM * (g - 1) + m
                if kk == BLOCK_AT[m] + 3:
                    sp.wait_ge(y_ready, slot + 2)
                    nc.sync.dma_start(yrows_t[bass.ds(slot, 1), :, :].rearrange("o p d -> (o p) d"),
                                      xs[:, m % 3, :]).then_inc(ys_out[m % 3], 16)

            body(0, first=True)
            sp.wait_ge(route_ready, 1)
            e = expert_of(0)
            load_w1(e, 0, 0)
            load_w1(e, 1, 1)
            load_w1(expert_of(1), 0, 2)
            sp.wait_ge(scattered, 16 * 2 * NT)
            load_rows(0, 0)
            load_rows(1, 1)
            for r in range(3):
                sp.sem_inc(ys_out[r], 16)
            for e in range(E // 2, E):
                load_w2(e)
            with sp.Fori(1, GROUPS - 1) as g:
                body(g)
            body(GROUPS - 1, last=True)
            sp.wait_ge(pj_free, pj_index(NCH, PJ_OUT) + 1)
            nc.sync.dma_start(mix_t[:, TT * (NCH - 1):TT * NCH, :], xres[:]).then_inc(mix_out, 16)
            for n in range(NT - TT, NT):
                load_mix(n)
            for n in range(NT - 4, NT):
                store_out(n)
            for b in range(4):
                sp.wait_ge(fin_out[b], 16 * NT // 4)
            for r in range(AHEAD):
                sp.wait_ge(xs_in[r], 16 * (SLOTS // 3 + 1))

        @block.gpsimd
        def _(pool):
            nc.gpsimd.memset(zeros, 0.0).then_inc(zero_ready, 1)
            nc.gpsimd.memset(ident[:], 0.0)
            nc.gpsimd.memset(half[:, 0, 0:2 * P], 0.0)
            nc.gpsimd.memset(pickf, 0.0).then_inc(const_ready, 1)
            pool.wait_ge(const_ready, 1)
            nc.gpsimd.affine_select(out=ident[:], in_=ident[:], compare_op=ALU.not_equal, fill=1.0, base=0,
                                    pattern=[[-1, P]], channel_multiplier=1)
            nc.gpsimd.affine_select(out=upper, in_=upper, compare_op=ALU.is_ge, fill=1.0, base=0,
                                    pattern=[[-1, P]], channel_multiplier=1)
            nc.gpsimd.memset(ones, 1.0).then_inc(const_ready, 1)
            nc.gpsimd.affine_select(out=pickf, in_=pickf, compare_op=ALU.not_equal, fill=1.0, base=0,
                                    pattern=[[-1, 2 * S]], channel_multiplier=1).then_inc(const_ready, 1)
            pool.wait_ge(const_ready, 3)
            nc.gpsimd.affine_select(out=pickf, in_=pickf, compare_op=ALU.not_equal, fill=1.0, base=-2 * S,
                                    pattern=[[-1, 2 * S]], channel_multiplier=1).then_inc(const_ready, 1)
            nc.gpsimd.iota(em8i, pattern=[[1, E]], base=-E, channel_multiplier=0).then_inc(const_ready, 1)
            nc.gpsimd.iota(sloti, pattern=[[1, SLOTS]], base=0, channel_multiplier=0).then_inc(const_ready, 1)

            def scatter(n, c):
                nc.gpsimd.indirect_dma_start(
                    out=rows_d, out_offset=bass.IndirectOffsetOnAxis(ap=pos[:, c, n:n + 1], axis=0),
                    in_=xn_all[:, n, :], in_offset=None).then_inc(scattered, 16)

            def gather(n):
                b = n % 4
                wait(pool, fin_ready, n - 3)
                for c in range(2):
                    nc.gpsimd.indirect_dma_start(
                        out=fin[:, 3 * b + 1 + c, :], out_offset=None, in_=yrows_d,
                        in_offset=bass.IndirectOffsetOnAxis(ap=pos[:, c, n:n + 1], axis=0)).then_inc(pick_in[b], 16)

            def make_u(g, kk):
                ci, k = kk // STEPS, kk % STEPS
                J, c, q = 2 * g + ci, k // NQ, k % NQ
                K = GS * g + kk
                if k == 0:
                    pool.wait_ge(dx_ready, J + 1)
                if c == 0:
                    pool.wait_ge(pj_free, spread_use(J, q, 1) + 1)
                wait(pool, scan_done, K - 1)
                nc.gpsimd.tensor_tensor(
                    u[:, kk % 2, :].rearrange("p (s t) -> p s t", s=SQ),
                    dx[:, ci, c, :].unsqueeze(1).broadcast_to([P, SQ, T]),
                    bc[:, 0, SQ * q:SQ * q + SQ, :], ALU.mult).then_inc(u_done, 1)

            def halve(g, kk):
                K = GS * g + kk
                pool.wait_ge(mul_done, K + 1)
                if not (isinstance(K, int) and K < GS):
                    pool.wait_ge(sum_done, K - 3)
                nc.gpsimd.tensor_tensor(half[:, kk % 4, :], prod[:, kk % 2, 0:SQ * T // 2],
                                        prod[:, kk % 2, SQ * T // 2:SQ * T], ALU.add).then_inc(half_done, 1)

            def gate(g, ci, c):
                J = 2 * g + ci
                if c == 0:
                    pool.wait_ge(z_ready, J + 1)
                pool.wait_ge(y_skip, CT * J + c + 1)
                nc.gpsimd.tensor_tensor(gz[:, ci % 2, c, :], xin[:, ci % 2, c, :], gz[:, ci % 2, c, :],
                                        ALU.mult).then_inc(gated, 1)

            def body(g, first=False, last=False):
                for kk in range(GS):
                    if not (last and kk == GS - 1):
                        make_u(g if kk < GS - 1 else g + 1, (kk + 1) % GS)
                    if kk == 0 and not first:
                        halve(g - 1, GS - 1)
                    if kk > 0 and not last and not (first and kk - 1 < FOLD_FROM):
                        halve(g, kk - 1)
                    if (first or last) and kk % 4 == 1 and not (first and kk == 1):
                        gate(g, (kk - 5) // STEPS, (kk // 4 - 1) % CT)
                    if not (first or last) and kk % 4 == 3:
                        gate(g, (kk - 7) // STEPS, (kk // 4 - 1) % CT)
                    if first and kk >= 4:
                        if kk == 4:
                            pool.wait_ge(route_ready, 1)
                            pool.wait_ge(zero_stored, 16 * (SLOTS // 8 + 1))
                        for i in range(3 * (kk - 4), min(3 * (kk - 3), 2 * NT)):
                            scatter(i // 2, i % 2)
                    if last and kk == 1:
                        for r in range(3):
                            pool.wait_ge(ys_out[r], 16 * (SLOTS // 3 + 1))
                            pool.wait_ge(w1_in[r], 16 * (2 * SLOTS // 3 + 1))
                    if last and kk >= 1:
                        gather(kk - 1)

            make_u(0, 0)
            body(0, first=True)
            with pool.Fori(1, GROUPS - 1) as g:
                body(g)
            body(GROUPS - 1, last=True)
            gate(GROUPS - 1, 1, CT - 1)
            gather(NT - 1)

        @block.scalar
        def _(act):
            def load(dst, src, s=w_load):
                nc.scalar.dma_start(dst, src).then_inc(s, 16)

            load(w_in[:], in_wT.rearrange("(k p) n -> p k n", p=P), w_first)
            load(gw[:], gate_w.rearrange("(k p) e -> p k e", p=P), w_first)
            load(a_neg[:], A_log.rearrange("(c p) s -> p c s", p=P))
            load(cw[:], conv_w.rearrange("(c p) o k -> p c (o k)", p=P))
            with nc.allow_non_contiguous_dma(reason="three vectors of 512"):
                load(cb[:], conv_b.rearrange("(c p) -> p c", p=P))
                load(dtb[:], dt_b.rearrange("(c p) -> p c", p=P))
                load(dskip[:], D_skip.rearrange("(c p) -> p c", p=P))
            load(xw_tmp, xp_w.rearrange("(c p) j -> p c j", p=P))
            load(dtw_tmp, dt_wT.rearrange("(c p) j -> p c j", p=P))
            for r in range(4):
                load(w_bc[:, :, 2 * S * r:2 * S * (r + 1)], bc_wT.rearrange("(c p) j -> p c j", p=P))
            load(w_out[:], out_wT.rearrange("(c p) n -> p c n", p=P))

            act.wait_ge(var_ready, 1)
            nc.scalar.activation(small[1], small[0], ACT.Sqrt).then_inc(root_ready, 1)

            def copy_T(J):
                act.wait_ge(head_T, J + 1)
                nc.scalar.activation(xnT_all[:, J].rearrange("p k t -> p (k t)"), hs_bank(J), ACT.Copy
                                     ).then_inc(head_Tcopy, 1)

            def copy_wm(jt):
                act.wait_ge(wm_full, jt + 1)
                nc.scalar.activation(w_dt[:, jt, :], (m0, m1)[jt % 2][:], ACT.Copy).then_inc(wm_free, 1)

            def copy_x(J, pair):
                act.wait_ge(pj_full, pj_ahead(J, PJ_X + pair) + 1)
                if pair == 0:
                    act.wait_ge(halo_ready, J + 1)
                nc.scalar.activation(xraw[:, 2 * pair:2 * pair + 2, TAPS - 1:],
                                     pj[:].rearrange("p (c t) -> p c t", c=2), ACT.Copy).then_inc(pj_free, 1)

            def copy_z(J, ci, pair):
                act.wait_ge(pj_full, pj_ahead(J, PJ_Z + pair) + 1)
                nc.scalar.activation(gz[:, ci, 2 * pair:2 * pair + 2, :],
                                     pj[:].rearrange("p (c t) -> p c t", c=2), ACT.Copy).then_inc(pj_free, 1)

            def silus(J, ci):
                act.wait_ge(pj_free, pj_ahead(J, PJ_Z + 1) + 1)
                nc.scalar.activation(gz[:, ci], gz[:, ci], ACT.Silu).then_inc(z_ready, 1)
                for c in range(CT):
                    act.wait_ge(conv_done, CT * J + c + 1)
                    nc.scalar.activation(xin[:, ci, c, :], xc[:, ci, c, :], ACT.Silu,
                                         bias=cb[:, c:c + 1]).then_inc(xin_ready, 1)
                nc.scalar.preload_act_table_set("natural_log_exp_and_others")

            def softplus(J, par):
                act.wait_ge(sp_min, J + 1)
                nc.scalar.activation(xc[:, par], xc[:, par], ACT.Exp).then_inc(sp_exp, 1)
                act.wait_ge(sp_exp, J + 1)
                nc.scalar.activation(xc[:, par], xc[:, par], ACT.Ln, bias=1.0).then_inc(sp_ln, 1)

            def spread_copy(J, q, first=False):
                for i in range(4):
                    act.wait_ge(pj_full, spread_use(J, q, i) + 1)
                    if i == 0 and not first:
                        act.wait_ge(u_done, STEPS * (J - 1) + STEPS - NQ + q + 1)
                        act.wait_ge(mul_done, STEPS * (J - 1) + STEPS - NQ + q + 1)
                    s0 = SQ * q + 2 * (i % 2)
                    nc.scalar.activation(bc[:, i // 2, s0:s0 + 2, :].rearrange("p s t -> p (s t)"),
                                         pj[:], ACT.Copy).then_inc(pj_free, 1)

            def decay(g, kk):
                ci, k = kk // STEPS, kk % STEPS
                J, c, q = 2 * g + ci, k // NQ, k % NQ
                if k == 0:
                    act.wait_ge(delta_ready, J + 1)
                wait(act, mul_done, GS * g + kk - 1)
                for s in range(SQ):
                    ins = nc.scalar.activation(hs[:, kk % 2, s * T:(s + 1) * T], delta[:, ci, c, :], ACT.Exp,
                                               scale=a_neg[:, c, SQ * q + s:SQ * q + s + 1])
                ins.then_inc(exp_done, 1)

            copy_T(0)
            copy_x(0, 0)
            copy_T(1)
            copy_T(2)
            copy_x(0, 1)
            copy_T(3)
            copy_T(4)
            for jt in range(CT):
                copy_wm(jt)
            copy_z(0, 0, 0)
            copy_z(0, 0, 1)
            silus(0, 0)
            for J in range(5, NCH):
                copy_T(J)
            act.wait_ge(w_load, 16 * N_W)
            nc.scalar.activation(a_neg[:], a_neg[:], ACT.Exp).then_inc(a_exp, 1)
            softplus(0, 0)
            spread_copy(0, 0, True)
            spread_copy(0, 1, True)
            act.wait_ge(a_ready, 1)
            decay(0, 0)

            def body(g, first=False, last=False):
                for kk in range(GS):
                    ci, k = kk // STEPS, kk % STEPS
                    J = 2 * g + ci
                    if not (last and kk == GS - 1):
                        decay(g if kk < GS - 1 else g + 1, (kk + 1) % GS)
                    if first and kk == 2:
                        act.wait_ge(gap_ready, 1)
                        nc.scalar.activation(small[3], small[3], ACT.Exp).then_inc(gap_exp, 1)
                    prep = not (last and ci == 1)
                    if k < 2:
                        spread_copy(J, 2 + k, first and ci == 0)
                    if prep:
                        if k == 2 or k == 3:
                            copy_x(J + 1, k - 2)
                        if k == 6 or k == 7:
                            copy_z(J + 1, 1 - ci, k - 6)
                        if k == 7:
                            silus(J + 1, 1 - ci)
                        if k == 11:
                            softplus(J + 1, 1 - ci)
                        if k >= 14:
                            spread_copy(J + 1, k - 14)
                    for m in range(GM):
                        if not (first or last) and kk == BLOCK_AT[m] + 1:
                            slot = GM * (g - 1) + m
                            act.wait_ge(y_full, slot + 1)
                            for hf in range(2):
                                act.wait_ge(h_full, 2 * slot + hf + 3)
                                nc.scalar.activation(
                                    hT[:, 4 * hf:4 * hf + 4, :].rearrange("p f n -> p (f n)"),
                                    (m1, m0)[hf][:], ACT.Gelu_apprx_tanh).then_inc(h_act, 1)
                            nc.scalar.preload_act_table_set("natural_log_exp_and_others")

            act.sem_inc(h_act, 2)
            body(0, first=True)
            with act.Fori(1, GROUPS - 1) as g:
                body(g)
            body(GROUPS - 1, last=True)

        @block.vector
        def _(dve):
            nc.vector.memset(xraw[:, :, 0:TAPS - 1], 0.0).then_inc(halo_ready, 1)
            dve.wait_ge(const_ready, N_CONST)
            nc.vector.tensor_copy(pick[:], pickf).then_inc(pick_ready, 1)
            nc.vector.tensor_copy(em8, em8i)
            nc.vector.tensor_copy(slotf, sloti)

            for n in range(NT + 2):
                if n < NT:
                    if n % 4 == 0:
                        dve.wait_ge(x_load[n // 4], 16)
                    nc.vector.bn_stats(stats[:, n, :], xn_all[:, n, :]).then_inc(stats_done, 1)
                if n >= 2:
                    dve.wait_ge(stats_done, n - 1)
                    nc.vector.bn_aggr(mv[:, n - 2, :], stats[:, n - 2, :]).then_inc(mean_done, 1)
            count = [0]

            def then(ins):
                count[0] += 1
                ins.then_inc(rt, 1)
                dve.wait_ge(rt, count[0])

            dve.wait_ge(mean_done, NT)
            nc.vector.tensor_scalar(small[0], mv[:, :, 1], EPS, None, ALU.add).then_inc(var_ready, 1)
            dve.wait_ge(root_ready, 1)
            then(nc.vector.reciprocal(small[2], small[1]))
            then(nc.vector.tensor_tensor(small[3], small[2], small[2], ALU.mult))
            then(nc.vector.tensor_tensor(small[3], small[3], small[0], ALU.mult))
            then(nc.vector.tensor_scalar(small[3], small[3], -0.5, 1.5, ALU.mult, ALU.add))
            then(nc.vector.tensor_tensor(rstd, small[2], small[3], ALU.mult))
            with dve.Fori(0, NT // 4) as i:
                for j in range(4):
                    row = xn_all[:, bass.ds(4 * i + j, 1), :].rearrange("p o d -> p (o d)")
                    nc.vector.tensor_scalar(row, row, mv[:, bass.ds(4 * i + j, 1), 0:1].rearrange("p o k -> p (o k)"),
                                            rstd[:, bass.ds(4 * i + j, 1)], ALU.subtract, ALU.mult
                                            ).then_inc(xn_ready, 1)

            def v(i):
                return w1s_flat[:, D * i:D * i + NT * E].rearrange("p (n e) -> p n e", e=E)

            lg = m1[:, 0:NT * E].rearrange("p (n e) -> p n e", e=E)
            shape = [P, NT, E]
            em8_b = em8.unsqueeze(1).broadcast_to(shape)
            def over_e(a):
                return a.unsqueeze(2).broadcast_to(shape)

            best, pick1, second, pick2 = small[0], v(2), small[1], v(4)

            def choose():
                dve.wait_ge(zero_stored, 16 * (SLOTS // 8 + 1))
                dve.wait_ge(gate_done, NT)
                then(nc.vector.tensor_reduce(best, lg, AX_X, ALU.max))
                then(nc.vector.tensor_tensor(v(0), lg, over_e(best), ALU.is_equal))
                then(nc.vector.tensor_tensor(v(1), v(0), em8_b, ALU.mult))
                then(nc.vector.tensor_reduce(small[2], v(1), AX_X, ALU.min))
                then(nc.vector.tensor_tensor(pick1, em8_b, over_e(small[2]), ALU.is_equal))
                then(nc.vector.scalar_tensor_tensor(out=v(3), in0=pick1, scalar=-3.0e38, in1=lg, op0=ALU.mult, op1=ALU.add))
                then(nc.vector.tensor_reduce(second, v(3), AX_X, ALU.max))
                then(nc.vector.tensor_tensor(v(0), v(3), over_e(second), ALU.is_equal))
                then(nc.vector.tensor_tensor(v(1), v(0), em8_b, ALU.mult))
                then(nc.vector.tensor_reduce(small[2], v(1), AX_X, ALU.min))
                then(nc.vector.tensor_tensor(pick2, em8_b, over_e(small[2]), ALU.is_equal))
                nc.vector.tensor_tensor(v(5), pick1, pick2, ALU.add).then_inc(mask_ready, 1)
                nc.vector.tensor_tensor(small[3], second, best, ALU.subtract).then_inc(gap_ready, 1)

            def place():
                dve.wait_ge(gap_exp, 1)
                then(nc.vector.tensor_scalar(small[4], small[3], 1.0, None, ALU.add))
                then(nc.vector.reciprocal(wgt[:, 0, :], small[4]))
                nc.vector.tensor_tensor(wgt[:, 1, :], small[3], wgt[:, 0, :], ALU.mult)
                dve.wait_ge(prefix_ready, 1)
                below = m0[:, 0:256].rearrange("p (n e) -> p n e", e=E)
                total = m0[:, 256:512].rearrange("p (n e) -> p n e", e=E)
                for e in range(E):
                    ins = nc.vector.tensor_tensor_scan(v(6)[:, :, e], ones[:, 0:NT], total[:, :, e], 0.0, ALU.mult, ALU.add)
                then(ins)
                then(nc.vector.tensor_tensor(v(7), v(6), total, ALU.subtract))
                then(nc.vector.tensor_tensor(v(7), v(7), below, ALU.add))
                then(nc.vector.tensor_scalar(e8[0].bitcast(I32), v(6)[:, NT - 1, :], float(P - 1), None, ALU.add))
                then(nc.vector.tensor_scalar(e8[1].bitcast(I32), e8[0].bitcast(I32), 7, None, ALU.arith_shift_right))
                then(nc.vector.tensor_copy(e8[2], e8[1].bitcast(I32)))
                then(nc.vector.tensor_tensor_scan(e8[3], ones[:, 0:E], e8[2], 0.0, ALU.mult, ALU.add))
                then(nc.vector.tensor_tensor(e8[4], e8[3], e8[2], ALU.subtract))
                then(nc.vector.tensor_scalar(e8[5], e8[4], float(P), None, ALU.mult))
                then(nc.vector.tensor_tensor(v(7), v(7), e8[5].unsqueeze(1).broadcast_to(shape), ALU.add))
                for c, one in ((0, pick1), (1, pick2)):
                    then(nc.vector.tensor_tensor(v(0), one, v(7), ALU.mult))
                    then(nc.vector.tensor_reduce(small[2], v(0), AX_X, ALU.add))
                    then(nc.vector.tensor_copy(pos[:, c, :], small[2]))
                ends = hT_flat[:, 0:SLOTS * E].rearrange("p (n e) -> p n e", e=E)
                then(nc.vector.tensor_tensor(ends, slotf.unsqueeze(2).broadcast_to([P, SLOTS, E]),
                                             e8[3].unsqueeze(1).broadcast_to([P, SLOTS, E]), ALU.is_ge))
                then(nc.vector.tensor_reduce(ends_sum, ends, AX_X, ALU.add))
                nc.vector.memset(slot_e[:, SLOTS:], 0)
                nc.vector.tensor_scalar(slot_e[:, 0:SLOTS], ends_sum, float(E - 1), None, ALU.min
                                        ).then_inc(route_ready, 1)


            def conv(J, par, c, first=False):
                if c % 2 == 0:
                    dve.wait_ge(pj_free, pj_ahead(J, PJ_X + c // 2) + 1)
                if first:
                    dve.wait_ge(wm_full, CT)
                nc.vector.tensor_scalar(xc[:, par, c, :], xraw[:, c, 0:T], cw[:, c, 0:1], None, ALU.mult
                                        ).then_inc(conv_t, 1)
                for tap in range(1, TAPS):
                    dve.wait_ge(conv_t, 3 * CT * J + 3 * c + tap)
                    ins = nc.vector.scalar_tensor_tensor(out=xc[:, par, c, :], in0=xraw[:, c, tap:tap + T],
                                                         scalar=cw[:, c, tap:tap + 1], in1=xc[:, par, c, :],
                                                         op0=ALU.mult, op1=ALU.add)
                    ins.then_inc(conv_done if tap == TAPS - 1 else conv_t, 1)
                if c == CT - 1:
                    nc.vector.tensor_copy(xraw[:, :, 0:TAPS - 1], xraw[:, :, T:T + TAPS - 1]).then_inc(halo_ready, 1)

            def copy_delta(J, ci, pair):
                dve.wait_ge(pj_full, pj_ahead(J, PJ_DT + pair) + 1)
                for j in range(2):
                    c = 2 * pair + j
                    ins = nc.vector.tensor_scalar(delta[:, ci, c, :], pj[:, T * j:T * j + T], dtb[:, c:c + 1], None,
                                                  ALU.add)
                ins.then_inc(pj_free, 1)

            def cut(J, ci):
                dve.wait_ge(pj_free, pj_ahead(J, PJ_DT + 1) + 1)
                nc.vector.tensor_scalar(xc[:, ci], delta[:, ci], SP_CUT, None, ALU.min).then_inc(sp_min, 1)

            def split_bc(J):
                dve.wait_ge(pj_full, pj_ahead(J, PJ_BC) + 1)
                nc.vector.tensor_copy(bcr[:], pj[:, 0:T]).then_inc(bcr_round, 1)
                dve.wait_ge(bcr_round, J + 1)
                ins = nc.vector.tensor_tensor(bcr[2 * S:4 * S, :], pj[2 * S:4 * S, 0:T],
                                              bcr[2 * S:4 * S, :].bitcast(F32), ALU.subtract)
                ins.then_inc(pj_free, 1)

            def finish_delta(J, ci):
                dve.wait_ge(sp_ln, J + 1)
                nc.vector.tensor_tensor(delta[:, ci], delta[:, ci], xc[:, ci], ALU.max).then_inc(delta_ready, 1)
                dve.wait_ge(delta_ready, J + 1)
                nc.vector.tensor_tensor(dx[:, ci], delta[:, ci], xin[:, ci], ALU.mult).then_inc(dx_ready, 1)

            def skip_term(g, ci, c):
                J = 2 * g + ci
                dve.wait_ge(sum_done, STEPS * J + NQ * c + NQ)
                nc.vector.scalar_tensor_tensor(out=xin[:, ci % 2, c, :], in0=xin[:, ci % 2, c, :], scalar=dskip[:, c:c + 1],
                                               in1=ysum[:, 0:T], op0=ALU.mult, op1=ALU.add).then_inc(y_skip, 1)

            def add_experts(n):
                b = n % 4
                acc = fin[:, 3 * b, :]
                dve.wait_ge(mix_in[b], 16 * (n // 4 + 1))
                dve.wait_ge(pick_in[b], 32 * (n // 4 + 1))
                nc.vector.scalar_tensor_tensor(out=acc, in0=fin[:, 3 * b + 1, :], scalar=wgt[:, 0, n:n + 1], in1=acc,
                                               op0=ALU.mult, op1=ALU.add).then_inc(fin_half, 1)
                dve.wait_ge(fin_half, n + 1)
                nc.vector.scalar_tensor_tensor(out=acc, in0=fin[:, 3 * b + 2, :], scalar=wgt[:, 1, n:n + 1], in1=acc,
                                               op0=ALU.mult, op1=ALU.add).then_inc(fin_ready, 1)

            def add_x(J):
                dve.wait_ge(pj_full, pj_index(J + 1, PJ_OUT) + 1)
                dve.wait_ge(xres_in, 16 * (J + 1))
                ins = nc.vector.tensor_tensor(xres[:].rearrange("p n d -> p (n d)"), pj[:],
                                              xres[:].rearrange("p n d -> p (n d)"), ALU.add)
                ins.then_inc(pj_free, 1)

            for c in range(CT):
                conv(0, 0, c, c == 0)
            dve.wait_ge(a_exp, 1)
            nc.vector.tensor_scalar(a_neg[:], a_neg[:], -1.0, None, ALU.mult).then_inc(a_ready, 1)
            copy_delta(0, 0, 0)
            copy_delta(0, 0, 1)
            cut(0, 0)
            split_bc(0)
            finish_delta(0, 0)

            def body(g, first=False, last=False):
                blocks = not (first or last)
                for kk in range(GS):
                    ci, k = kk // STEPS, kk % STEPS
                    J, c, q = 2 * g + ci, k // NQ, k % NQ
                    K = GS * g + kk
                    prep = not (last and ci == 1)
                    dve.wait_ge(exp_done, K + 1)
                    dve.wait_ge(u_done, K + 1)
                    at_zero = first and ci == 0
                    if not at_zero:
                        dve.wait_ge(carry_saved, K - STEPS + 1)
                    for s in range(SQ):
                        h = hs[:, kk % 2, s * T:(s + 1) * T]
                        start = 0.0 if at_zero else carry[:, c, SQ * q + s:SQ * q + s + 1]
                        ins = nc.vector.tensor_tensor_scan(h, h, u[:, kk % 2, s * T:(s + 1) * T], start, ALU.mult, ALU.add)
                    ins.then_inc(scan_done, 1)

                    if (first or last) and kk % 4 == 1 and not (first and kk == 1):
                        skip_term(g, (kk - 5) // STEPS, (kk // 4 - 1) % CT)
                    if blocks and kk % 4 == 3:
                        skip_term(g, (kk - 7) // STEPS, (kk // 4 - 1) % CT)
                    dve.wait_ge(scan_done, K + 1)
                    nc.vector.tensor_copy(carry[:, c, SQ * q:SQ * q + SQ],
                                          hs[:, kk % 2, :].rearrange("p (s t) -> p s t", s=SQ)[:, :, T - 1]
                                          ).then_inc(carry_saved, 1)
                    if c == 0:
                        dve.wait_ge(pj_free, spread_use(J, q, 3) + 1)
                    if blocks or (first and kk - 2 >= FOLD_FROM) or (last and kk < 2):
                        dve.wait_ge(half_done, K - 1 - FOLD_FROM)
                    else:
                        wait(dve, sum_done, K - 1)
                    nc.vector.tensor_tensor(prod[:, kk % 2, :], hs[:, kk % 2, :],
                                            bc[:, 1, SQ * q:SQ * q + SQ, :].rearrange("p s t -> p (s t)"),
                                            ALU.mult).then_inc(mul_done, 1)

                    if first and kk == 1:
                        choose()
                    if first and kk == 2:
                        place()
                    for m in range(GM):
                        if blocks and kk == BLOCK_AT[m]:
                            slot = GM * (g - 1) + m
                            dve.wait_ge(xsT_full, slot + 1)
                            dve.wait_ge(h_full, 2 * slot + 2)
                            nc.vector.tensor_copy(xsT[:].rearrange("p k n -> p (k n)"), m1[:, 0:KD * P]
                                                  ).then_inc(xsT_ready, 1)
                    if k == 5 and not at_zero:
                        add_x(J - 1)
                    if prep:
                        if 3 <= k < 3 + CT:
                            conv(J + 1, 1 - ci, k - 3)
                        if k == 8 or k == 10:
                            copy_delta(J + 1, 1 - ci, 0 if k == 8 else 1)
                        if k == 10:
                            cut(J + 1, 1 - ci)
                        if k == 11:
                            split_bc(J + 1)
                        if k == 13:
                            finish_delta(J + 1, 1 - ci)
                    if last and kk >= 3:
                        add_experts(kk - 3)
                    for m in range(GM):
                        if blocks and kk == BLOCK_AT[m] + 3:
                            slot = GM * (g - 1) + m
                            dve.wait_ge(y_full, slot + 2)
                            nc.vector.tensor_copy(xs[:, m % 3, :], m0[:, 0:D]).then_inc(y_ready, 1)

            dve.sem_inc(y_ready, 1)
            body(0, first=True)
            with dve.Fori(1, GROUPS - 1) as g:
                body(g)
            body(GROUPS - 1, last=True)
            skip_term(GROUPS - 1, 1, CT - 1)
            add_x(NCH - 1)
            for n in range(GS - 3, NT):
                add_experts(n)

        @block.tensor
        def _(pe):
            def head_transpose(J):
                wait(pe, head_Tcopy, J - 3)
                for tt in range(TT):
                    pe.wait_ge(xn_ready, TT * J + tt + 1)
                    for kd in range(KD):
                        ins = nc.tensor.transpose(hs_bank(J)[:, kd * T + tt * P:kd * T + tt * P + P],
                                                  xn_all[:, TT * J + tt, kd * P:kd * P + P], ident[:])
                ins.then_inc(head_T, 1)

            def merge(jt):
                wait(pe, wm_free, jt - 1)
                for it in range(CT):
                    ins = nc.tensor.matmul((m0, m1)[jt % 2][:], xw_tmp[:, it, P * jt:P * jt + P], dtw_tmp[:, it, :],
                                           start=(it == 0), stop=(it == CT - 1))
                ins.then_inc(wm_full, 1)

            def logits(n):
                if n == 0:
                    pe.wait_ge(head_Tcopy, NCH)
                    pe.wait_ge(wm_free, CT)
                for kd in range(KD):
                    ins = nc.tensor.matmul(m1[:, E * n:E * n + E], xnT_all[:, n // TT, kd, P * (n % TT):P * (n % TT) + P],
                                           gw[:, kd, :], start=(kd == 0), stop=(kd == KD - 1))
                ins.then_inc(gate_done, 1)

            def prefixes():
                pe.wait_ge(mask_ready, 1)
                mask = w1s_flat[:, 5 * D:5 * D + NT * E]
                nc.tensor.matmul(m0[:, 0:256], upper, mask, start=True, stop=True)
                nc.tensor.matmul(m0[:, 256:512], ones, mask, start=True, stop=True).then_inc(prefix_ready, 1)

            def in_proj(J, r, m):
                wait(pe, pj_free, pj_ahead(J, r))
                rows = xnT
                if isinstance(J, int) and J == 0:
                    rows = xnT_all[:, 0]
                elif m == 0:
                    pe.wait_ge(xnT_in, 16 * J)
                for j in range(2):
                    for kd in range(KD):
                        ins = nc.tensor.matmul(pj[:, T * j:T * j + T], w_in[:, kd, P * (m + j):P * (m + j + 1)],
                                               rows[:, kd, :], start=(kd == 0), stop=(kd == KD - 1))
                ins.then_inc(pj_full, 1)

            def delta_proj(J, ci, pair):
                wait(pe, pj_free, pj_ahead(J, PJ_DT + pair))
                if pair == 0:
                    pe.wait_ge(xin_ready, CT * (J + 1))
                for j in range(2):
                    e0 = P * (2 * pair + j)
                    for c in range(CT):
                        ins = nc.tensor.matmul(pj[:, T * j:T * j + T], w_dt[:, c, e0:e0 + P], xin[:, ci, c, :],
                                               start=(c == 0), stop=(c == CT - 1))
                ins.then_inc(pj_full, 1)

            def bc_proj(J, ci):
                wait(pe, pj_free, pj_ahead(J, PJ_BC))
                for c in range(CT):
                    ins = nc.tensor.matmul(pj[:, 0:T], w_bc[:, c, :], xin[:, ci, c, :],
                                           start=(c == 0), stop=(c == CT - 1))
                ins.then_inc(pj_full, 1)

            def spread(J, q, i):
                wait(pe, pj_free, spread_use(J, q, i))
                for j in range(2):
                    row = S * (i // 2) + SQ * q + 2 * (i % 2) + j
                    ins = nc.tensor.matmul(pj[:, T * j:T * j + T], pick[:, row:row + 1].broadcast_to([P, P]), bcr[:],
                                           start=True, stop=True)
                ins.then_inc(pj_full, 1)

            def out_proj(J, ci):
                wait(pe, pj_free, pj_index(J + 1, PJ_OUT))
                pe.wait_ge(gated, CT * (J + 1))
                for tt in range(TT):
                    for c in range(CT):
                        ins = nc.tensor.matmul(pj[:, D * tt:D * tt + D], gz[:, ci, c, P * tt:P * tt + P], w_out[:, c, :],
                                               start=(c == 0), stop=(c == CT - 1))
                ins.then_inc(pj_full, 1)

            def sum_states(g, kk, folded):
                K = GS * g + kk
                q = kk % NQ
                if folded:
                    pe.wait_ge(half_done, K - FOLD_FROM + 1)
                else:
                    pe.wait_ge(mul_done, K + 1)
                if q == 0:
                    wait(pe, y_skip, 2 * CT * g + kk // NQ)
                n = 2 if folded else 4
                for j in range(n):
                    src = half[:, kk % 4, T * j:T * j + T] if folded else prod[:, kk % 2, T * j:T * j + T]
                    ins = nc.tensor.matmul(ysum[:, 0:T], ident[:], src,
                                           start=(q == 0 and j == 0), stop=(q == NQ - 1 and j == n - 1))
                ins.then_inc(sum_done, 1)

            def block_T(g, m):
                slot = GM * (g - 1) + m
                pe.wait_ge(xs_in[m % 3], 16 * (4 * (g - 1) + m // 3 + 1))
                pe.wait_ge(h_act, 2 * slot + 1)
                for kd in range(KD):
                    ins = nc.tensor.transpose(m1[:, P * kd:P * kd + P], xs[:, m % 3, P * kd:P * kd + P], ident[:])
                ins.then_inc(xsT_full, 1)

            def block_h(g, m, i):
                slot = GM * (g - 1) + m
                hf = i // 2
                if i == 0:
                    pe.wait_ge(xsT_ready, slot + 1)
                if i == 2:
                    pe.wait_ge(y_ready, slot + 1)
                hi = 2 * m + hf
                if i % 2 == 0:
                    pe.wait_ge(w1_in[hi % 3], 16 * (8 * (g - 1) + hi // 3 + 1))
                for f in (2 * (i % 2), 2 * (i % 2) + 1):
                    for kd in range(KD):
                        ins = nc.tensor.matmul((m1, m0)[hf][:, P * f:P * f + P], w1s[:, hi % 3, kd, P * f:P * f + P],
                                               xsT[:, kd, :], start=(kd == 0), stop=(kd == KD - 1))
                if i % 2 == 1:
                    ins.then_inc(h_full, 1)

            def block_y(g, m, i, e):
                slot = GM * (g - 1) + m
                if i == 0:
                    pe.wait_ge(h_act, 2 * slot + 4)
                for f in (2 * i, 2 * i + 1):
                    ins = nc.tensor.matmul(m0[:, 0:D], hT[:, f, :], w2s[:, bass.ds(e * (FT * D) + f * D, D)],
                                           start=(f == 0), stop=(f == FT - 1))
                if i == 3:
                    ins.then_inc(y_full, 1)

            def block_quarter(g, kk, i, e):
                for m in range(GM):
                    if kk == BLOCK_AT[m] + 1:
                        block_h(g, m, i)
                    if kk == BLOCK_AT[m] + 2:
                        block_y(g, m, i, e)

            pe.wait_ge(const_ready, N_CONST)
            pe.wait_ge(w_first, 32)
            head_transpose(0)
            pe.wait_ge(head_Tcopy, 1)
            in_proj(0, PJ_X, 0)
            head_transpose(1)
            head_transpose(2)
            in_proj(0, PJ_X + 1, 2)
            head_transpose(3)
            head_transpose(4)
            in_proj(0, PJ_Z, 4)
            pe.wait_ge(w_load, 16 * N_W)
            for jt in range(CT):
                merge(jt)
            in_proj(0, PJ_Z + 1, 6)
            for J in range(5, NCH):
                head_transpose(J)
            delta_proj(0, 0, 0)
            for n in range(4):
                logits(n)
            delta_proj(0, 0, 1)
            for n in range(4, 8):
                logits(n)
            bc_proj(0, 0)
            pe.wait_ge(pick_ready, 1)
            for i in range(8):
                for n in range(8 + 3 * i, 11 + 3 * i):
                    logits(n)
                if i == 0:
                    pe.wait_ge(pj_free, pj_ahead(0, PJ_BC) + 1)
                spread(0, i // 4, i % 4)

            def body(g, first=False, last=False):
                blocks = not (first or last)
                for kk in range(GS):
                    ci, k = kk // STEPS, kk % STEPS
                    J = 2 * g + ci
                    prep = not (last and ci == 1)
                    e = None
                    if blocks:
                        for m in range(GM):
                            if kk == BLOCK_AT[m] + 2:
                                e = pe.value_load(slot_e[0:1, bass.ds(GM * (g - 1) + m, 1)], min_val=0, max_val=E - 1)
                    if first and kk == 2:
                        prefixes()
                    if blocks:
                        for m in range(GM):
                            if kk == BLOCK_AT[m]:
                                block_T(g, m)
                    if prep and (k == 2 or k == 3):
                        in_proj(J + 1, PJ_X + k - 2, 2 * (k - 2))
                    if k == 5 and not (first and ci == 0):
                        out_proj(J - 1, 1 - ci)
                    if prep:
                        if k == 6:
                            in_proj(J + 1, PJ_Z, 4)
                        if k == 7:
                            in_proj(J + 1, PJ_Z + 1, 6)
                        if k == 8 or k == 10:
                            delta_proj(J + 1, 1 - ci, 0 if k == 8 else 1)
                        if k == 11:
                            bc_proj(J + 1, 1 - ci)
                    for i in range(4):
                        if k < 2:
                            spread(J, 2 + k, i)
                        if prep and k >= 14:
                            spread(J + 1, k - 14, i)
                        if blocks:
                            block_quarter(g, kk, i, e)
                    if blocks:
                        if kk < 3:
                            sum_states(g - 1, kk - 3 + GS, True)
                        else:
                            sum_states(g, kk - 3, True)
                    if first:
                        if 1 <= kk <= FOLD_FROM:
                            sum_states(g, kk - 1, False)
                        if kk - 3 >= FOLD_FROM:
                            sum_states(g, kk - 3, True)
                    if last:
                        if kk == 0:
                            sum_states(g - 1, GS - 3, True)
                            sum_states(g - 1, GS - 2, True)
                        if kk == 1:
                            sum_states(g - 1, GS - 1, True)
                        if kk >= 1:
                            sum_states(g, kk - 1, False)

            pe.sem_inc(h_full, 2)
            pe.sem_inc(y_full, 1)
            body(0, first=True)
            pe.wait_ge(w2_load, 16 * E)
            with pe.Fori(1, GROUPS - 1) as g:
                body(g)
            body(GROUPS - 1, last=True)
            sum_states(GROUPS - 1, GS - 1, False)
            out_proj(NCH - 1, 1)


_INS = {
    "x": (L, D), "in_wT": (D, 2 * DI), "conv_w": (DI, 1, TAPS), "conv_b": (DI,), "xp_w": (DI, DI),
    "bc_wT": (DI, 2 * S), "dt_wT": (DI, DI), "dt_b": (DI,), "A_log": (DI, S), "D_skip": (DI,),
    "out_wT": (DI, D), "gate_w": (D, E), "w1": (2 * E, P, KD * HF), "w2": (E, P, FT * D),
}


def kernel(L0_attn_x, L0_attn_in_proj_w, L0_attn_conv_w, L0_attn_conv_b, L0_attn_x_proj_w, L0_attn_dt_proj_w,
           L0_attn_dt_proj_b, L0_attn_A_log, L0_attn_D, L0_attn_out_proj_w, L0_ffn_gate_w, L0_ffn_w1, L0_ffn_w2):
    import concourse.bacc as bacc
    from concourse.bass_utils import run_bass_kernel_spmd

    w1 = np.asarray(L0_ffn_w1).reshape(E, KD, P, 2, HF).transpose(0, 3, 2, 1, 4).reshape(2 * E, P, KD * HF)
    w2 = np.asarray(L0_ffn_w2).reshape(E, FT, P, D).transpose(0, 2, 1, 3).reshape(E, P, FT * D)
    xp = np.asarray(L0_attn_x_proj_w)
    arrays = {
        "x": np.asarray(L0_attn_x).reshape(L, D), "in_wT": np.asarray(L0_attn_in_proj_w).T,
        "conv_w": L0_attn_conv_w, "conv_b": L0_attn_conv_b, "xp_w": xp[:DI], "bc_wT": xp[DI:].T,
        "dt_wT": np.asarray(L0_attn_dt_proj_w).T, "dt_b": L0_attn_dt_proj_b, "A_log": L0_attn_A_log,
        "D_skip": L0_attn_D, "out_wT": np.asarray(L0_attn_out_proj_w).T, "gate_w": L0_ffn_gate_w, "w1": w1, "w2": w2,
    }
    arrays = {k: np.ascontiguousarray(a) for k, a in arrays.items()}
    nc = bacc.Bacc("TRN2", target_bir_lowering=False, num_devices=1)
    aps = [nc.dram_tensor(k, shape, F32, kind="ExternalInput").ap() for k, shape in _INS.items()]
    out = nc.dram_tensor("out", (L, D), F32, kind="ExternalOutput").ap()
    mamba_moe_kernel(nc, *aps, out)
    r = run_bass_kernel_spmd(nc, [arrays], core_ids=[0])
    return r.results[0]["out"].reshape(1, L, D)
```

```python
from contextlib import ExitStack

import numpy as np

import concourse.bass as bass
from concourse import mybir

ALU = mybir.AluOpType
ACT = mybir.ActivationFunctionType
F32 = mybir.dt.float32
F32R = mybir.dt.float32r
I32 = mybir.dt.int32
AX_X = mybir.AxisListType.X

P = 128
L = 4096
D = 256
KD = D // P
DI = 512
CT = DI // P
S = 16
TAPS = 4
T = 256
NCH = L // T
TT = T // P
NT = L // P
SQ = 4
NQ = S // SQ
STEPS = CT * NQ
E = 8
F = 1024
FT = F // P
HF = F // 2
SLOTS = 72
GROUPS = NCH // 2
GS = 2 * STEPS
GM = SLOTS // (GROUPS - 2)

H_AT = [0, 4, 7, 10, 12, 14, 16, 20, 23, 26, 28, 30]
X_AT = (2, 3)
OUT_AT = 5
Z_AT = (6, 7)
DELTA_AT = (8, 10)
BC_AT = 11
CONV_AT = 3
SILU_AT = 7
SOFTPLUS_AT = 11
DX_AT = 13
CHOOSE_AT = 5
SCATTER_AT = (7, 29)
ACT_COPIES = (1, 2, 3)
XN_POOL = (6, 14)
FOLD_FROM = GS - 4
AHEAD = 2
EPS = 1e-5
SP_CUT = 30.0

PJ_X, PJ_OUT, PJ_Z, PJ_DT, PJ_BC, PJ_SPREAD = 8, 10, 11, 13, 15, 16
PJ_HEAD = 15


def pj_index(J, r):
    if isinstance(J, int) and J == 0 and r < PJ_OUT:
        return PJ_HEAD + r
    if isinstance(J, int) and J >= NCH - 1 and r == PJ_OUT:
        return PJ_HEAD - 1 + 24 * (NCH - 1) + PJ_X + J - (NCH - 1)
    return PJ_HEAD - 1 + 24 * J + r


def pj_ahead(J, r):
    if isinstance(J, int) and J == 0:
        return {PJ_X: 0, PJ_X + 1: 1, PJ_Z: 2, PJ_Z + 1: 3, PJ_DT: 4, PJ_DT + 1: 5, PJ_BC: 6}.get(r, r - PJ_SPREAD + 7)
    return pj_index(J - 1, r)


def spread_use(J, q, i):
    if q < 2:
        return pj_ahead(J, PJ_SPREAD + 4 * q + i)
    return pj_index(J, 4 * (q - 2) + i)




def wait(eng, sem, value):
    if isinstance(value, int) and value <= 0:
        return
    eng.wait_ge(sem, value)


def mamba_moe_kernel(nc, x, in_wT, conv_w, conv_b, xp_w, bc_wT, dt_wT, dt_b, A_log, D_skip, out_wT,
                     gate_w, w1, w2, out):
    with ExitStack() as ctx:
        def sb(name, shape, dt=F32):
            return ctx.enter_context(nc.sbuf_tensor(name, shape, dt))

        def sem(name):
            return ctx.enter_context(nc.semaphore(name))

        xnT_d = nc.dram_tensor("xnT_d", [NCH, P, KD * T], F32, kind="Internal").ap()
        rows_d = nc.dram_tensor("rows_d", [(SLOTS + 8) * P, D], F32, kind="Internal").ap()
        yrows_d = nc.dram_tensor("yrows_d", [SLOTS * P, D], F32, kind="Internal").ap()
        mix_d = nc.dram_tensor("mix_d", [L, D], F32, kind="Internal").ap()

        w2s = sb("w2s", [P, E * FT * D])
        w1s = sb("w1s", [P, 3, KD, HF])
        w_in = sb("w_in", [P, KD, 2 * DI])
        w_dt = sb("w_dt", [P, CT, DI])
        w_bc = sb("w_bc", [P, CT, P])
        w_out = sb("w_out", [P, CT, D])
        ident = sb("ident", [P, P])
        pick = sb("pick", [P, 2 * S], F32R)
        a_neg = sb("a_neg", [P, CT, S])
        cw = sb("cw", [P, CT, TAPS])
        cb = sb("cb", [P, CT])
        dtb = sb("dtb", [P, CT])
        dskip = sb("dskip", [P, CT])
        gw = sb("gw", [P, KD, E])

        bc = sb("bc", [P, 2, S, T])
        xnT = sb("xnT", [P, KD, T])
        xres = sb("xres", [P, TT, D])
        xraw = sb("xraw", [P, CT, TAPS - 1 + T])
        xin = sb("xin", [P, 2, CT, T])
        delta = sb("delta", [P, 2, CT, T])
        dx = sb("dx", [P, 2, CT, T])
        gz = sb("gz", [P, 2, CT, T])
        u = sb("u", [P, 2, SQ * T])
        prod = sb("prod", [P, 2, SQ * T])
        half = sb("half", [P, 4, SQ * T // 2])
        carry = sb("carry", [P, CT, S])
        bcr = sb("bcr", [P, T], F32R)

        xs = sb("xs", [P, 3, D])
        xsT = sb("xsT", [P, KD, P])
        hT = sb("hT", [P, FT, P])

        pos = sb("pos", [P, 2, NT], I32)
        wgt = sb("wgt", [P, 2, NT])
        slot_e = sb("slot_e", [P, SLOTS + AHEAD], I32)

        xc = dx
        xnT_all = w2s[:, 0:L * KD].rearrange("p (j k t) -> p j k t", k=KD, t=T)
        xn_all = w2s[:, L * KD:].rearrange("p (n d) -> p n d", d=D)
        xw_tmp = delta.rearrange("p a c t -> p (a c t)").rearrange("p (c j) -> p c j", c=CT)
        dtw_tmp = dx.rearrange("p a c t -> p (a c t)").rearrange("p (c j) -> p c j", c=CT)
        w1s_flat = w1s.rearrange("p r k f -> p (r k f)")
        hT_flat = hT.rearrange("p f n -> p (f n)")
        zeros = w1s_flat[:, 0:8 * D]
        stats = w1s_flat[:, 8 * D:8 * D + 6 * NT].rearrange("p (n k) -> p n k", k=6)
        mv = w1s_flat[:, 9 * D:9 * D + 2 * NT].rearrange("p (n k) -> p n k", k=2)
        rstd = w1s_flat[:, 10 * D:10 * D + NT]
        ends_sum = w1s_flat[:, 11 * D:11 * D + SLOTS]
        fin = w1s_flat.rearrange("p (b d) -> p b d", d=D)
        upper = half[:, 0, 0:P]
        ones = half[:, 0, P:2 * P]
        pickf = half[:, 1, 64:96]
        em8i = half[:, 1, 96:104].bitcast(I32)
        em8 = half[:, 1, 104:112]
        sloti = half[:, 1, 112:112 + SLOTS].bitcast(I32)
        slotf = half[:, 1, 192:192 + SLOTS]
        small = [half[:, 1, 272 + 32 * i:304 + 32 * i] for i in range(6)]
        e8 = [half[:, 1, 464 + 8 * i:472 + 8 * i] for i in range(6)]

        hs = ctx.enter_context(nc.psum_tensor("hs", [P, 2, SQ * T], F32))
        ysum = ctx.enter_context(nc.psum_tensor("ysum", [P, 512], F32))
        pj = ctx.enter_context(nc.psum_tensor("pj", [P, 512], F32))
        m0 = ctx.enter_context(nc.psum_tensor("m0", [P, 512], F32))
        m1 = ctx.enter_context(nc.psum_tensor("m1", [P, 512], F32))

        def bank(m, what):
            return (m0, m1)[(m + (what == 1)) % 2]

        def spread_bank(other, i):
            return pj if other is None or i % 2 == 0 else other

        def hs_bank(J):
            return hs[:, J // 2 % 2, 512 * (J % 2):512 * (J % 2) + 512]

        w_merge, w_first, w_load, w2_load = sem("w_merge"), sem("w_first"), sem("w_load"), sem("w2_load")
        x_load = [sem(f"x_load{i}") for i in range(8)]
        zero_ready, zero_stored = sem("zero_ready"), sem("zero_stored")
        const_ready, pick_ready = sem("const_ready"), sem("pick_ready")
        a_exp, a_ready = sem("a_exp"), sem("a_ready")
        stats_done, mean_done, var_ready, root_ready, rstd_ready = (
            sem("stats_done"), sem("mean_done"), sem("var_ready"), sem("root_ready"), sem("rstd_ready"))
        xn_dve, xn_pool = sem("xn_dve"), sem("xn_pool")
        head_T, head_Tcopy, head_Tstore = sem("head_T"), sem("head_Tcopy"), sem("head_Tstore")
        gate_done, wm_full, wm_free = sem("gate_done"), sem("wm_full"), sem("wm_free")
        rt, mask_ready, prefix_ready, gap_ready, gap_exp = (
            sem("rt"), sem("mask_ready"), sem("prefix_ready"), sem("gap_ready"), sem("gap_exp"))
        route_ready, scattered = sem("route_ready"), sem("scattered")
        exp_done, u_done, own_u = sem("exp_done"), sem("u_done"), sem("own_u")
        scan_done, carry_saved, mul_done = sem("scan_done"), sem("carry_saved"), sem("mul_done")
        half_done, quarter_done, sum_done = sem("half_done"), sem("quarter_done"), sem("sum_done")
        y_skip, gated = sem("y_skip"), sem("gated")
        pj_full, pj_free = sem("pj_full"), sem("pj_free")
        xnT_in, xres_in, mix_out = sem("xnT_in"), sem("xres_in"), sem("mix_out")
        halo_ready, conv_t, conv_done, xin_ready = (
            sem("halo_ready"), sem("conv_t"), sem("conv_done"), sem("xin_ready"))
        sp_min, sp_exp, sp_ln, delta_ready, dx_ready = (
            sem("sp_min"), sem("sp_exp"), sem("sp_ln"), sem("delta_ready"), sem("dx_ready"))
        bcr_round, z_ready = sem("bcr_round"), sem("z_ready")
        w1_in = [sem(f"w1_in{i}") for i in range(3)]
        xs_in = [sem(f"xs_in{i}") for i in range(3)]
        ys_out = [sem(f"ys_out{i}") for i in range(3)]
        xsT_full, xsT_ready, h_full, h_act, y_full, y_ready = (
            sem("xsT_full"), sem("xsT_ready"), sem("h_full"), sem("h_act"), sem("y_full"), sem("y_ready"))
        pick_in = [sem(f"pick_in{i}") for i in range(4)]
        mix_in = [sem(f"mix_in{i}") for i in range(4)]
        fin_half, fin_ready = sem("fin_half"), sem("fin_ready")
        fin_out = [sem(f"fin_out{i}") for i in range(4)]

        x_t = x.rearrange("(n p) d -> p n d", p=P)
        mix_t = mix_d.rearrange("(n p) d -> p n d", p=P)
        out_t = out.rearrange("(n p) d -> p n d", p=P)
        rows_t = rows_d.rearrange("(n p) d -> n p d", p=P)
        yrows_t = yrows_d.rearrange("(n p) d -> n p d", p=P)
        N_W = 10
        N_CONST = 6

        def shared_u(g, kk):
            return isinstance(g, int) and g == 0 and SCATTER_AT[0] <= kk < SCATTER_AT[1] and kk % 2 == 1

        block = ctx.enter_context(nc.Block())

        @block.sync
        def _(sp):
            for i in range(8):
                nc.sync.dma_start(xn_all[:, 4 * i:4 * i + 4, :], x_t[:, 4 * i:4 * i + 4, :]).then_inc(x_load[i], 16)
            sp.wait_ge(w_load, 16 * N_W)
            sp.wait_ge(zero_ready, 1)
            zview = rows_d.rearrange("(b p r) d -> b p (r d)", p=P, r=8)
            for b in range(SLOTS // 8 + 1):
                nc.sync.dma_start(zview[b], zeros).then_inc(zero_stored, 16)
            for J in range(1, NCH):
                sp.wait_ge(head_Tcopy, J + 1)
                nc.sync.dma_start(xnT_d[J], xnT_all[:, J].rearrange("p k t -> p (k t)")).then_inc(head_Tstore, 16)
            sp.wait_ge(head_Tstore, 16 * (NCH - 1))

            def load_xnT(J):
                nc.sync.dma_start(xnT[:].rearrange("p k t -> p (k t)"),
                                  xnT_d[bass.ds(J, 1), :, :].rearrange("o p n -> (o p) n")).then_inc(xnT_in, 16)

            def expert_of(slot):
                return sp.value_load(slot_e[0:1, bass.ds(slot, 1)], min_val=0, max_val=E - 1)

            def load_w1(e, hf, ring):
                nc.sync.dma_start(w1s[:, ring].rearrange("p k f -> p (k f)"),
                                  w1[bass.ds(2 * e + hf, 1), :, :].rearrange("o p n -> (o p) n")
                                  ).then_inc(w1_in[ring], 16)

            def load_rows(slot, ring):
                nc.sync.dma_start(xs[:, ring, :], rows_t[bass.ds(slot, 1), :, :].rearrange("o p d -> (o p) d")
                                  ).then_inc(xs_in[ring], 16)

            def load_w2(e):
                nc.sync.dma_start(w2s[:, e * FT * D:(e + 1) * FT * D], w2[e]).then_inc(w2_load, 16)

            def load_mix(n):
                b = n % 4
                sp.wait_ge(mix_out, 16 * (n // TT + 1))
                if n == 0:
                    for r in range(3):
                        sp.wait_ge(w1_in[r], 16 * (2 * SLOTS // 3 + 1))
                    sp.wait_ge(h_full, 2 * SLOTS + 2)
                wait(sp, fin_out[b], 16 * (n // 4))
                nc.sync.dma_start(fin[:, 3 * b, :], mix_t[:, n, :]).then_inc(mix_in[b], 16)

            def store_out(n):
                sp.wait_ge(fin_ready, n + 1)
                src = fin[:, 3 * (n % 4), :] if n < NT - TT else xres[:, n % TT, :]
                nc.sync.dma_start(out_t[:, n, :], src).then_inc(fin_out[n % 4], 16)

            load_xnT(1)
            sp.wait_ge(gate_done, NT)
            for e in range(E // 2):
                load_w2(e)

            def body(g, first=False, last=False):
                blocks = not (first or last)
                for kk in range(GS):
                    ci, k = kk // STEPS, kk % STEPS
                    J = 2 * g + ci
                    if k == 8 and not last:
                        sp.wait_ge(pj_full, pj_index(J, PJ_Z + 1) + 1)
                        load_xnT(J + 2)
                    if k == 7:
                        if not (first and ci == 0):
                            sp.wait_ge(pj_free, pj_index(J, PJ_OUT) + 1)
                            nc.sync.dma_start(mix_t[:, bass.ds(TT * (J - 1), TT), :], xres[:]).then_inc(mix_out, 16)
                    if k == 10:
                        wait(sp, mix_out, 16 * J)
                        nc.sync.dma_start(xres[:], x_t[:, bass.ds(TT * J, TT), :]).then_inc(xres_in, 16)
                    if blocks:
                        for m in range(GM):
                            block_loads(g, kk, m)
                        for m in range(GM):
                            store_block(g, kk, m)
                        for m in range(GM):
                            block_rows(g, kk, m)
                    if first and kk == SCATTER_AT[1]:
                        sp.wait_ge(route_ready, 1)
                        e = expert_of(0)
                        load_w1(e, 0, 0)
                        load_w1(e, 1, 1)
                        load_w1(expert_of(1), 0, 2)
                        sp.wait_ge(scattered, 16 * 2 * NT)
                        load_rows(0, 0)
                        load_rows(1, 1)
                        for e in range(E // 2, E):
                            load_w2(e)
                    if last:
                        if kk >= 4:
                            store_out(kk - 4)
                        if kk < NT - TT:
                            load_mix(kk)

            def block_loads(g, kk, m):
                slot = GM * (g - 1) + m
                if kk == H_AT[m]:
                    e, e_next = expert_of(slot + 1), expert_of(slot + 2)
                    sp.wait_ge(h_full, 2 * slot + 3)
                    load_w1(e, 1, (2 * m + 3) % 3)
                    sp.wait_ge(h_full, 2 * slot + 4)
                    load_w1(e_next, 0, (2 * m + 4) % 3)

            def block_rows(g, kk, m):
                slot = GM * (g - 1) + m
                if kk == H_AT[m]:
                    sp.wait_ge(ys_out[(m + 2) % 3], 16 * (4 * (g - 1) + (m + 2) // 3 + 1))
                    load_rows(slot + 2, (m + 2) % 3)

            def store_block(g, kk, m):
                slot = GM * (g - 1) + m
                if kk == min(H_AT[m] + 2, GS - 1):
                    sp.wait_ge(y_ready, slot + 2)
                    nc.sync.dma_start(yrows_t[bass.ds(slot, 1), :, :].rearrange("o p d -> (o p) d"),
                                      xs[:, m % 3, :]).then_inc(ys_out[m % 3], 16)

            for r in range(3):
                sp.sem_inc(ys_out[r], 16)
            body(0, first=True)
            with sp.Fori(1, GROUPS - 1) as g:
                body(g)
            body(GROUPS - 1, last=True)
            for n in range(NT - 4, NT):
                store_out(n)
            for b in range(4):
                sp.wait_ge(fin_out[b], 16 * NT // 4)
            for r in range(AHEAD):
                sp.wait_ge(xs_in[r], 16 * (SLOTS // 3 + 1))

        @block.gpsimd
        def _(pool):
            nc.gpsimd.memset(zeros, 0.0).then_inc(zero_ready, 1)
            nc.gpsimd.memset(ident[:], 0.0)
            nc.gpsimd.memset(half[:, 0, 0:2 * P], 0.0)
            nc.gpsimd.memset(pickf, 0.0).then_inc(const_ready, 1)
            pool.wait_ge(const_ready, 1)
            nc.gpsimd.affine_select(out=ident[:], in_=ident[:], compare_op=ALU.not_equal, fill=1.0, base=0,
                                    pattern=[[-1, P]], channel_multiplier=1)
            nc.gpsimd.affine_select(out=upper, in_=upper, compare_op=ALU.is_ge, fill=1.0, base=0,
                                    pattern=[[-1, P]], channel_multiplier=1)
            nc.gpsimd.memset(ones, 1.0).then_inc(const_ready, 1)
            nc.gpsimd.affine_select(out=pickf, in_=pickf, compare_op=ALU.not_equal, fill=1.0, base=0,
                                    pattern=[[-1, 2 * S]], channel_multiplier=1).then_inc(const_ready, 1)
            pool.wait_ge(const_ready, 3)
            nc.gpsimd.affine_select(out=pickf, in_=pickf, compare_op=ALU.not_equal, fill=1.0, base=-2 * S,
                                    pattern=[[-1, 2 * S]], channel_multiplier=1).then_inc(const_ready, 1)
            nc.gpsimd.iota(em8i, pattern=[[1, E]], base=-E, channel_multiplier=0).then_inc(const_ready, 1)
            nc.gpsimd.iota(sloti, pattern=[[1, SLOTS]], base=0, channel_multiplier=0).then_inc(const_ready, 1)

            pool.wait_ge(rstd_ready, 1)
            for n in range(*XN_POOL):
                nc.gpsimd.tensor_scalar(xn_all[:, n, :], xn_all[:, n, :], mv[:, n, 0:1], rstd[:, n:n + 1],
                                        ALU.subtract, ALU.mult).then_inc(xn_pool, 1)

            def scatter(n, c):
                nc.gpsimd.indirect_dma_start(
                    out=rows_d, out_offset=bass.IndirectOffsetOnAxis(ap=pos[:, c, n:n + 1], axis=0),
                    in_=xn_all[:, n, :], in_offset=None).then_inc(scattered, 16)

            def gather(n):
                b = n % 4
                wait(pool, fin_ready, n - 3)
                for c in range(2):
                    nc.gpsimd.indirect_dma_start(
                        out=fin[:, 3 * b + 1 + c, :], out_offset=None, in_=yrows_d,
                        in_offset=bass.IndirectOffsetOnAxis(ap=pos[:, c, n:n + 1], axis=0)).then_inc(pick_in[b], 16)

            def make_u(g, kk):
                states = SQ // 2 if shared_u(g, kk) else SQ
                ci, k = kk // STEPS, kk % STEPS
                J, c, q = 2 * g + ci, k // NQ, k % NQ
                K = GS * g + kk
                if k == 0:
                    pool.wait_ge(dx_ready, J + 1)
                if c == 0:
                    pool.wait_ge(pj_free, spread_use(J, q, 1) + 1)
                wait(pool, scan_done, K - 1)
                nc.gpsimd.tensor_tensor(
                    u[:, kk % 2, 0:states * T].rearrange("p (s t) -> p s t", s=states),
                    dx[:, ci, c, :].unsqueeze(1).broadcast_to([P, states, T]),
                    bc[:, 0, SQ * q:SQ * q + states, :], ALU.mult).then_inc(u_done, 1)

            def halve(g, kk):
                K = GS * g + kk
                pool.wait_ge(mul_done, K + 1)
                if not (isinstance(K, int) and K < GS):
                    pool.wait_ge(sum_done, K - 3)
                nc.gpsimd.tensor_tensor(half[:, kk % 4, :], prod[:, kk % 2, 0:SQ * T // 2],
                                        prod[:, kk % 2, SQ * T // 2:SQ * T], ALU.add).then_inc(half_done, 1)

            def quarter(g, kk):
                pool.wait_ge(half_done, GS * g + kk - FOLD_FROM + 1)
                nc.gpsimd.tensor_tensor(half[:, kk % 4, 0:T], half[:, kk % 4, 0:T], half[:, kk % 4, T:2 * T],
                                        ALU.add).then_inc(quarter_done, 1)

            def gate(g, ci, c):
                J = 2 * g + ci
                if c == 0:
                    pool.wait_ge(z_ready, J + 1)
                pool.wait_ge(y_skip, CT * J + c + 1)
                nc.gpsimd.tensor_tensor(gz[:, ci % 2, c, :], xin[:, ci % 2, c, :], gz[:, ci % 2, c, :],
                                        ALU.mult).then_inc(gated, 1)

            def body(g, first=False, last=False):
                for kk in range(GS):
                    before = (g, kk - 1) if kk > 0 else (g - 1, GS - 1)
                    folded = not ((last and kk > 0) or (first and kk - 1 < FOLD_FROM))
                    if folded:
                        halve(*before)
                    if not (first or last) and kk % 4 == 3:
                        gate(g, (kk - 7) // STEPS, (kk // 4 - 1) % CT)
                    if not (last and kk == GS - 1):
                        make_u(g if kk < GS - 1 else g + 1, (kk + 1) % GS)
                    if folded:
                        quarter(*before)
                    if (first or last) and kk % 4 == 1 and not (first and kk == 1):
                        gate(g, (kk - 5) // STEPS, (kk // 4 - 1) % CT)
                    if first and SCATTER_AT[0] <= kk < SCATTER_AT[1]:
                        if kk == SCATTER_AT[0]:
                            pool.wait_ge(route_ready, 1)
                            pool.wait_ge(zero_stored, 16 * (SLOTS // 8 + 1))
                        steps, done = SCATTER_AT[1] - SCATTER_AT[0], kk - SCATTER_AT[0]
                        for i in range(2 * NT * done // steps, 2 * NT * (done + 1) // steps):
                            scatter(i // 2, i % 2)
                    if last and kk == 1:
                        for r in range(3):
                            pool.wait_ge(ys_out[r], 16 * (SLOTS // 3 + 1))
                            pool.wait_ge(w1_in[r], 16 * (2 * SLOTS // 3 + 1))
                    if last and kk >= 1:
                        gather(kk - 1)

            make_u(0, 0)
            body(0, first=True)
            with pool.Fori(1, GROUPS - 1) as g:
                body(g)
            body(GROUPS - 1, last=True)
            gate(GROUPS - 1, 1, CT - 1)
            gather(NT - 1)

        @block.scalar
        def _(act):
            def load(dst, src, s=w_load):
                nc.scalar.dma_start(dst, src).then_inc(s, 16)

            load(xw_tmp, xp_w.rearrange("(c p) j -> p c j", p=P), w_merge)
            load(dtw_tmp, dt_wT.rearrange("(c p) j -> p c j", p=P), w_merge)
            load(w_in[:], in_wT.rearrange("(k p) n -> p k n", p=P), w_first)
            load(gw[:], gate_w.rearrange("(k p) e -> p k e", p=P), w_first)
            load(a_neg[:], A_log.rearrange("(c p) s -> p c s", p=P))
            load(cw[:], conv_w.rearrange("(c p) o k -> p c (o k)", p=P))
            with nc.allow_non_contiguous_dma(reason="three vectors of 512"):
                load(cb[:], conv_b.rearrange("(c p) -> p c", p=P))
                load(dtb[:], dt_b.rearrange("(c p) -> p c", p=P))
                load(dskip[:], D_skip.rearrange("(c p) -> p c", p=P))
            for r in range(4):
                load(w_bc[:, :, 2 * S * r:2 * S * (r + 1)], bc_wT.rearrange("(c p) j -> p c j", p=P))
            load(w_out[:], out_wT.rearrange("(c p) n -> p c n", p=P))

            def copy_T(J):
                act.wait_ge(head_T, J + 1)
                nc.scalar.activation(xnT_all[:, J].rearrange("p k t -> p (k t)"), hs_bank(J), ACT.Copy
                                     ).then_inc(head_Tcopy, 1)

            def copy_wm(jt):
                act.wait_ge(wm_full, jt + 1)
                nc.scalar.activation(w_dt[:, jt, :], (m0, m1)[jt % 2][:], ACT.Copy).then_inc(wm_free, 1)

            def copy_x(J, pair):
                act.wait_ge(pj_full, pj_ahead(J, PJ_X + pair) + 1)
                if pair == 0:
                    act.wait_ge(halo_ready, J + 1)
                nc.scalar.activation(xraw[:, 2 * pair:2 * pair + 2, TAPS - 1:],
                                     pj[:].rearrange("p (c t) -> p c t", c=2), ACT.Copy).then_inc(pj_free, 1)

            def copy_z(J, ci, pair):
                act.wait_ge(pj_full, pj_ahead(J, PJ_Z + pair) + 1)
                nc.scalar.activation(gz[:, ci, 2 * pair:2 * pair + 2, :],
                                     pj[:].rearrange("p (c t) -> p c t", c=2), ACT.Copy).then_inc(pj_free, 1)

            def silus(J, ci):
                act.wait_ge(pj_free, pj_ahead(J, PJ_Z + 1) + 1)
                nc.scalar.activation(gz[:, ci], gz[:, ci], ACT.Silu).then_inc(z_ready, 1)
                for c in range(CT):
                    act.wait_ge(conv_done, CT * J + c + 1)
                    nc.scalar.activation(xin[:, ci, c, :], xc[:, ci, c, :], ACT.Silu,
                                         bias=cb[:, c:c + 1]).then_inc(xin_ready, 1)
                nc.scalar.preload_act_table_set("natural_log_exp_and_others")

            def softplus(J, par):
                act.wait_ge(sp_min, J + 1)
                nc.scalar.activation(xc[:, par], xc[:, par], ACT.Exp).then_inc(sp_exp, 1)
                act.wait_ge(sp_exp, J + 1)
                nc.scalar.activation(xc[:, par], xc[:, par], ACT.Ln, bias=1.0).then_inc(sp_ln, 1)

            def spread_copy(J, q, i, other=None, first=False):
                act.wait_ge(pj_full, spread_use(J, q, i) + 1)
                if i == 0 and not first:
                    act.wait_ge(u_done, STEPS * (J - 1) + STEPS - NQ + q + 1)
                    act.wait_ge(mul_done, STEPS * (J - 1) + STEPS - NQ + q + 1)
                s0 = SQ * q + 2 * (i % 2)
                nc.scalar.activation(bc[:, i // 2, s0:s0 + 2, :].rearrange("p s t -> p (s t)"),
                                     spread_bank(other, i)[:], ACT.Copy).then_inc(pj_free, 1)

            def gelu(slot, m, hf):
                if hf == 0:
                    act.wait_ge(y_full, slot + 1)
                act.wait_ge(h_full, 2 * slot + hf + 3)
                nc.scalar.activation(hT[:, 4 * hf:4 * hf + 4, :].rearrange("p f n -> p (f n)"),
                                     bank(m, hf)[:], ACT.Gelu_apprx_tanh).then_inc(h_act, 1)

            def decay(g, kk):
                ci, k = kk // STEPS, kk % STEPS
                J, c, q = 2 * g + ci, k // NQ, k % NQ
                if k == 0:
                    act.wait_ge(delta_ready, J + 1)
                wait(act, mul_done, GS * g + kk - 1)
                for s in range(SQ):
                    ins = nc.scalar.activation(hs[:, kk % 2, s * T:(s + 1) * T], delta[:, ci, c, :], ACT.Exp,
                                               scale=a_neg[:, c, SQ * q + s:SQ * q + s + 1])
                ins.then_inc(exp_done, 1)

            copy_wm(0)
            copy_wm(1)
            act.wait_ge(var_ready, 1)
            nc.scalar.activation(small[1], small[0], ACT.Sqrt).then_inc(root_ready, 1)
            copy_wm(2)
            copy_wm(3)
            copy_T(0)
            copy_x(0, 0)
            copy_T(1)
            copy_x(0, 1)
            copy_T(2)
            copy_z(0, 0, 0)
            copy_T(3)
            copy_z(0, 0, 1)
            act.wait_ge(w_load, 16 * N_W)
            silus(0, 0)
            for J in range(4, 8):
                copy_T(J)
            nc.scalar.activation(a_neg[:], a_neg[:], ACT.Exp).then_inc(a_exp, 1)
            for J in range(8, 12):
                copy_T(J)
            softplus(0, 0)
            for i in range(8):
                if i < 4:
                    copy_T(12 + i)
                spread_copy(0, i // 4, i % 4, m0, True)
                if i == 3:
                    act.wait_ge(a_ready, 1)
                    decay(0, 0)

            def body(g, first=False, last=False):
                for kk in range(GS):
                    ci, k = kk // STEPS, kk % STEPS
                    J = 2 * g + ci
                    if not (last and kk == GS - 1):
                        decay(g if kk < GS - 1 else g + 1, (kk + 1) % GS)
                    if first and kk == CHOOSE_AT + 1:
                        act.wait_ge(gap_ready, 1)
                        nc.scalar.activation(small[3], small[3], ACT.Exp).then_inc(gap_exp, 1)
                    prep = not (last and ci == 1)
                    if prep:
                        if k in X_AT:
                            copy_x(J + 1, X_AT.index(k))
                        if k in Z_AT:
                            copy_z(J + 1, 1 - ci, Z_AT.index(k))
                        if k == SILU_AT:
                            silus(J + 1, 1 - ci)
                        if k == SOFTPLUS_AT:
                            softplus(J + 1, 1 - ci)
                    m = H_AT.index(kk) if not (first or last) and kk in H_AT else None
                    for i in range(4):
                        if i == 1 and m is not None:
                            nc.scalar.preload_act_table_set("gelu_apprx_tanh_and_others")
                        if first or last:
                            if k < 2:
                                spread_copy(J, 2 + k, i, m0 if first and ci == 0 else m1, first and ci == 0)
                            if prep and k >= 14:
                                spread_copy(J + 1, k - 14, i, m1)
                        elif i in ACT_COPIES:
                            if k < 2:
                                spread_copy(J, 2 + k, i)
                            if k >= 14:
                                spread_copy(J + 1, k - 14, i)
                        if i == 1 and m is not None:
                            gelu(GM * (g - 1) + m, m, 0)
                    if m is not None:
                        gelu(GM * (g - 1) + m, m, 1)
                        nc.scalar.preload_act_table_set("natural_log_exp_and_others")

            act.sem_inc(h_act, 2)
            body(0, first=True)
            with act.Fori(1, GROUPS - 1) as g:
                body(g)
            body(GROUPS - 1, last=True)

        @block.vector
        def _(dve):
            nc.vector.memset(xraw[:, :, 0:TAPS - 1], 0.0).then_inc(halo_ready, 1)
            dve.wait_ge(const_ready, N_CONST)
            nc.vector.tensor_copy(pick[:], pickf).then_inc(pick_ready, 1)
            nc.vector.tensor_copy(em8, em8i)
            nc.vector.tensor_copy(slotf, sloti)

            for n in range(NT + 2):
                if n < NT:
                    if n % 4 == 0:
                        dve.wait_ge(x_load[n // 4], 16)
                    nc.vector.bn_stats(stats[:, n, :], xn_all[:, n, :]).then_inc(stats_done, 1)
                if n >= 2:
                    dve.wait_ge(stats_done, n - 1)
                    nc.vector.bn_aggr(mv[:, n - 2, :], stats[:, n - 2, :]).then_inc(mean_done, 1)
            count = [0]

            def then(ins):
                count[0] += 1
                ins.then_inc(rt, 1)
                dve.wait_ge(rt, count[0])

            dve.wait_ge(mean_done, NT)
            nc.vector.tensor_scalar(small[0], mv[:, :, 1], EPS, None, ALU.add).then_inc(var_ready, 1)
            dve.wait_ge(root_ready, 1)
            then(nc.vector.reciprocal(small[2], small[1]))
            then(nc.vector.tensor_tensor(small[3], small[2], small[2], ALU.mult))
            then(nc.vector.tensor_tensor(small[3], small[3], small[0], ALU.mult))
            then(nc.vector.tensor_scalar(small[3], small[3], -0.5, 1.5, ALU.mult, ALU.add))
            nc.vector.tensor_tensor(rstd, small[2], small[3], ALU.mult).then_inc(rstd_ready, 1)
            dve.wait_ge(rstd_ready, 1)

            def normalize(tiles):
                for n in tiles:
                    nc.vector.tensor_scalar(xn_all[:, n, :], xn_all[:, n, :], mv[:, n, 0:1], rstd[:, n:n + 1],
                                            ALU.subtract, ALU.mult).then_inc(xn_dve, 1)

            normalize(range(XN_POOL[0]))

            def v(i):
                return w1s_flat[:, D * i:D * i + NT * E].rearrange("p (n e) -> p n e", e=E)

            lg = m1[:, 0:NT * E].rearrange("p (n e) -> p n e", e=E)
            shape = [P, NT, E]
            em8_b = em8.unsqueeze(1).broadcast_to(shape)
            def over_e(a):
                return a.unsqueeze(2).broadcast_to(shape)

            best, pick1, second, pick2 = small[0], v(2), small[1], v(4)

            def choose():
                dve.wait_ge(zero_stored, 16 * (SLOTS // 8 + 1))
                dve.wait_ge(gate_done, NT)
                then(nc.vector.tensor_reduce(best, lg, AX_X, ALU.max))
                then(nc.vector.tensor_tensor(v(0), lg, over_e(best), ALU.is_equal))
                then(nc.vector.tensor_tensor(v(1), v(0), em8_b, ALU.mult))
                then(nc.vector.tensor_reduce(small[2], v(1), AX_X, ALU.min))
                then(nc.vector.tensor_tensor(pick1, em8_b, over_e(small[2]), ALU.is_equal))
                then(nc.vector.scalar_tensor_tensor(out=v(3), in0=pick1, scalar=-3.0e38, in1=lg,
                                                    op0=ALU.mult, op1=ALU.add))
                then(nc.vector.tensor_reduce(second, v(3), AX_X, ALU.max))
                then(nc.vector.tensor_tensor(v(0), v(3), over_e(second), ALU.is_equal))
                then(nc.vector.tensor_tensor(v(1), v(0), em8_b, ALU.mult))
                then(nc.vector.tensor_reduce(small[2], v(1), AX_X, ALU.min))
                then(nc.vector.tensor_tensor(pick2, em8_b, over_e(small[2]), ALU.is_equal))
                nc.vector.tensor_tensor(v(5), pick1, pick2, ALU.add).then_inc(mask_ready, 1)
                nc.vector.tensor_tensor(small[3], second, best, ALU.subtract).then_inc(gap_ready, 1)

            def place():
                dve.wait_ge(gap_exp, 1)
                then(nc.vector.tensor_scalar(small[4], small[3], 1.0, None, ALU.add))
                then(nc.vector.reciprocal(wgt[:, 0, :], small[4]))
                nc.vector.tensor_tensor(wgt[:, 1, :], small[3], wgt[:, 0, :], ALU.mult)
                dve.wait_ge(prefix_ready, 1)
                below = m0[:, 0:256].rearrange("p (n e) -> p n e", e=E)
                total = m0[:, 256:512].rearrange("p (n e) -> p n e", e=E)
                for e in range(E):
                    ins = nc.vector.tensor_tensor_scan(v(6)[:, :, e], ones[:, 0:NT], total[:, :, e], 0.0,
                                                     ALU.mult, ALU.add)
                then(ins)
                then(nc.vector.tensor_tensor(v(7), v(6), total, ALU.subtract))
                then(nc.vector.tensor_tensor(v(7), v(7), below, ALU.add))
                then(nc.vector.tensor_scalar(e8[0].bitcast(I32), v(6)[:, NT - 1, :], float(P - 1), None, ALU.add))
                then(nc.vector.tensor_scalar(e8[1].bitcast(I32), e8[0].bitcast(I32), 7, None, ALU.arith_shift_right))
                then(nc.vector.tensor_copy(e8[2], e8[1].bitcast(I32)))
                then(nc.vector.tensor_tensor_scan(e8[3], ones[:, 0:E], e8[2], 0.0, ALU.mult, ALU.add))
                then(nc.vector.tensor_tensor(e8[4], e8[3], e8[2], ALU.subtract))
                then(nc.vector.tensor_scalar(e8[5], e8[4], float(P), None, ALU.mult))
                then(nc.vector.tensor_tensor(v(7), v(7), e8[5].unsqueeze(1).broadcast_to(shape), ALU.add))
                for c, one in ((0, pick1), (1, pick2)):
                    then(nc.vector.tensor_tensor(v(0), one, v(7), ALU.mult))
                    then(nc.vector.tensor_reduce(small[2], v(0), AX_X, ALU.add))
                    then(nc.vector.tensor_copy(pos[:, c, :], small[2]))
                ends = hT_flat[:, 0:SLOTS * E].rearrange("p (n e) -> p n e", e=E)
                then(nc.vector.tensor_tensor(ends, slotf.unsqueeze(2).broadcast_to([P, SLOTS, E]),
                                             e8[3].unsqueeze(1).broadcast_to([P, SLOTS, E]), ALU.is_ge))
                then(nc.vector.tensor_reduce(ends_sum, ends, AX_X, ALU.add))
                nc.vector.memset(slot_e[:, SLOTS:], 0)
                nc.vector.tensor_scalar(slot_e[:, 0:SLOTS], ends_sum, float(E - 1), None, ALU.min
                                        ).then_inc(route_ready, 1)


            def conv(J, par, c, first=False):
                if c % 2 == 0:
                    dve.wait_ge(pj_free, pj_ahead(J, PJ_X + c // 2) + 1)
                if first:
                    dve.wait_ge(wm_full, CT)
                    dve.wait_ge(w_load, 16 * N_W)
                nc.vector.tensor_scalar(xc[:, par, c, :], xraw[:, c, 0:T], cw[:, c, 0:1], None, ALU.mult
                                        ).then_inc(conv_t, 1)
                for tap in range(1, TAPS):
                    dve.wait_ge(conv_t, 3 * CT * J + 3 * c + tap)
                    ins = nc.vector.scalar_tensor_tensor(out=xc[:, par, c, :], in0=xraw[:, c, tap:tap + T],
                                                         scalar=cw[:, c, tap:tap + 1], in1=xc[:, par, c, :],
                                                         op0=ALU.mult, op1=ALU.add)
                    ins.then_inc(conv_done if tap == TAPS - 1 else conv_t, 1)
                if c == CT - 1:
                    nc.vector.tensor_copy(xraw[:, :, 0:TAPS - 1], xraw[:, :, T:T + TAPS - 1]).then_inc(halo_ready, 1)

            def copy_delta(J, ci, pair):
                dve.wait_ge(pj_full, pj_ahead(J, PJ_DT + pair) + 1)
                for j in range(2):
                    c = 2 * pair + j
                    ins = nc.vector.tensor_scalar(delta[:, ci, c, :], pj[:, T * j:T * j + T], dtb[:, c:c + 1], None,
                                                  ALU.add)
                ins.then_inc(pj_free, 1)

            def cut(J, ci):
                dve.wait_ge(pj_free, pj_ahead(J, PJ_DT + 1) + 1)
                nc.vector.tensor_scalar(xc[:, ci], delta[:, ci], SP_CUT, None, ALU.min).then_inc(sp_min, 1)

            def split_bc(J):
                dve.wait_ge(pj_full, pj_ahead(J, PJ_BC) + 1)
                nc.vector.tensor_copy(bcr[:], pj[:, 0:T]).then_inc(bcr_round, 1)
                dve.wait_ge(bcr_round, J + 1)
                ins = nc.vector.tensor_tensor(bcr[2 * S:4 * S, :], pj[2 * S:4 * S, 0:T],
                                              bcr[2 * S:4 * S, :].bitcast(F32), ALU.subtract)
                ins.then_inc(pj_free, 1)

            def finish_delta(J, ci):
                dve.wait_ge(sp_ln, J + 1)
                nc.vector.tensor_tensor(delta[:, ci], delta[:, ci], xc[:, ci], ALU.max).then_inc(delta_ready, 1)
                dve.wait_ge(delta_ready, J + 1)
                nc.vector.tensor_tensor(dx[:, ci], delta[:, ci], xin[:, ci], ALU.mult).then_inc(dx_ready, 1)
                if isinstance(J, int):
                    dve.wait_ge(dx_ready, J + 1)

            def spread_copy(J, q, i):
                dve.wait_ge(pj_full, spread_use(J, q, i) + 1)
                s0 = SQ * q + 2 * (i % 2)
                nc.vector.tensor_copy(bc[:, i // 2, s0:s0 + 2, :].rearrange("p s t -> p (s t)"), pj[:]
                                      ).then_inc(pj_free, 1)

            def skip_term(g, ci, c):
                J = 2 * g + ci
                dve.wait_ge(sum_done, STEPS * J + NQ * c + NQ)
                nc.vector.scalar_tensor_tensor(out=xin[:, ci % 2, c, :], in0=xin[:, ci % 2, c, :],
                                               scalar=dskip[:, c:c + 1], in1=ysum[:, 0:T],
                                               op0=ALU.mult, op1=ALU.add).then_inc(y_skip, 1)

            def add_experts(n):
                b = n % 4
                if n < NT - TT:
                    acc = fin[:, 3 * b, :]
                    dve.wait_ge(mix_in[b], 16 * (n // 4 + 1))
                else:
                    acc = xres[:, n % TT, :]
                    dve.wait_ge(pj_free, pj_index(NCH, PJ_OUT) + 1)
                dve.wait_ge(pick_in[b], 32 * (n // 4 + 1))
                nc.vector.scalar_tensor_tensor(out=acc, in0=fin[:, 3 * b + 1, :], scalar=wgt[:, 0, n:n + 1], in1=acc,
                                               op0=ALU.mult, op1=ALU.add).then_inc(fin_half, 1)
                dve.wait_ge(fin_half, n + 1)
                nc.vector.scalar_tensor_tensor(out=acc, in0=fin[:, 3 * b + 2, :], scalar=wgt[:, 1, n:n + 1], in1=acc,
                                               op0=ALU.mult, op1=ALU.add).then_inc(fin_ready, 1)

            def copy_xsT(slot, m):
                dve.wait_ge(xsT_full, slot + 1)
                dve.wait_ge(h_full, 2 * slot + 2)
                nc.vector.tensor_copy(xsT[:].rearrange("p k n -> p (k n)"), bank(m, "T")[:, 0:KD * P]
                                      ).then_inc(xsT_ready, 1)

            def copy_y(slot, m):
                dve.wait_ge(y_full, slot + 2)
                nc.vector.tensor_copy(xs[:, m % 3, :], bank(m, "y")[:, 0:D]).then_inc(y_ready, 1)

            def add_x(J):
                dve.wait_ge(pj_full, pj_index(J + 1, PJ_OUT) + 1)
                dve.wait_ge(xres_in, 16 * (J + 1))
                ins = nc.vector.tensor_tensor(xres[:].rearrange("p n d -> p (n d)"), pj[:],
                                              xres[:].rearrange("p n d -> p (n d)"), ALU.add)
                ins.then_inc(pj_free, 1)

            for c in range(CT):
                conv(0, 0, c, c == 0)
            normalize(range(XN_POOL[1], NT))
            dve.wait_ge(a_exp, 1)
            nc.vector.tensor_scalar(a_neg[:], a_neg[:], -1.0, None, ALU.mult).then_inc(a_ready, 1)
            copy_delta(0, 0, 0)
            copy_delta(0, 0, 1)
            cut(0, 0)
            split_bc(0)
            finish_delta(0, 0)

            def body(g, first=False, last=False):
                blocks = not (first or last)
                for kk in range(GS):
                    ci, k = kk // STEPS, kk % STEPS
                    J, c, q = 2 * g + ci, k // NQ, k % NQ
                    K = GS * g + kk
                    prep = not (last and ci == 1)
                    at_zero = first and ci == 0
                    if shared_u(g, kk):
                        if c == 0:
                            dve.wait_ge(pj_free, spread_use(J, q, 1) + 1)
                        nc.vector.tensor_tensor(
                            u[:, kk % 2, SQ * T // 2:].rearrange("p (s t) -> p s t", s=SQ // 2),
                            dx[:, ci, c, :].unsqueeze(1).broadcast_to([P, SQ // 2, T]),
                            bc[:, 0, SQ * q + SQ // 2:SQ * q + SQ, :], ALU.mult).then_inc(own_u, 1)
                        dve.wait_ge(own_u, len([i for i in range(kk + 1) if shared_u(g, i)]))
                    for i in range(4):
                        if blocks and i not in ACT_COPIES and k < 2:
                            spread_copy(J, 2 + k, i)
                        if blocks and i not in ACT_COPIES and k >= 14:
                            spread_copy(J + 1, k - 14, i)
                    dve.wait_ge(exp_done, K + 1)
                    dve.wait_ge(u_done, K + 1)
                    if not at_zero:
                        dve.wait_ge(carry_saved, K - STEPS + 1)
                    for s in range(SQ):
                        h = hs[:, kk % 2, s * T:(s + 1) * T]
                        start = 0.0 if at_zero else carry[:, c, SQ * q + s:SQ * q + s + 1]
                        ins = nc.vector.tensor_tensor_scan(h, h, u[:, kk % 2, s * T:(s + 1) * T], start,
                                                         ALU.mult, ALU.add)
                    ins.then_inc(scan_done, 1)

                    for m in range(GM - 1):
                        if blocks and kk == H_AT[m] + 2:
                            copy_y(GM * (g - 1) + m, m)
                    if (first or last) and kk % 4 == 1 and not (first and kk == 1):
                        skip_term(g, (kk - 5) // STEPS, (kk // 4 - 1) % CT)
                    if blocks and kk % 4 == 3:
                        skip_term(g, (kk - 7) // STEPS, (kk // 4 - 1) % CT)
                    dve.wait_ge(scan_done, K + 1)
                    nc.vector.tensor_copy(carry[:, c, SQ * q:SQ * q + SQ],
                                          hs[:, kk % 2, :].rearrange("p (s t) -> p s t", s=SQ)[:, :, T - 1]
                                          ).then_inc(carry_saved, 1)
                    if c == 0:
                        dve.wait_ge(pj_free, spread_use(J, q, 3) + 1)
                    if blocks or (first and kk - 2 >= FOLD_FROM) or (last and kk < 2):
                        dve.wait_ge(half_done, K - 1 - FOLD_FROM)
                    else:
                        wait(dve, sum_done, K - 1)
                    nc.vector.tensor_tensor(prod[:, kk % 2, :], hs[:, kk % 2, :],
                                            bc[:, 1, SQ * q:SQ * q + SQ, :].rearrange("p s t -> p (s t)"),
                                            ALU.mult).then_inc(mul_done, 1)

                    if first and kk == CHOOSE_AT:
                        choose()
                    if first and kk == CHOOSE_AT + 1:
                        place()
                    if blocks and kk + 1 in H_AT:
                        copy_xsT(GM * (g - 1) + H_AT.index(kk + 1), H_AT.index(kk + 1))
                    if kk == GS - 1 and not last:
                        copy_xsT(GM * g, 0)
                    if k == OUT_AT and not at_zero:
                        add_x(J - 1)
                    if prep:
                        if CONV_AT <= k < CONV_AT + CT:
                            conv(J + 1, 1 - ci, k - CONV_AT)
                        if k in DELTA_AT:
                            copy_delta(J + 1, 1 - ci, DELTA_AT.index(k))
                        if k == DELTA_AT[1]:
                            cut(J + 1, 1 - ci)
                        if k == BC_AT:
                            split_bc(J + 1)
                        if k == DX_AT:
                            finish_delta(J + 1, 1 - ci)
                    if last and kk >= 3:
                        add_experts(kk - 3)
                    if blocks and kk == GS - 1:
                        copy_y(GM * (g - 1) + GM - 1, GM - 1)

            dve.sem_inc(y_ready, 1)
            body(0, first=True)
            with dve.Fori(1, GROUPS - 1) as g:
                body(g)
            body(GROUPS - 1, last=True)
            skip_term(GROUPS - 1, 1, CT - 1)
            add_x(NCH - 1)
            for n in range(GS - 3, NT):
                add_experts(n)

        @block.tensor
        def _(pe):
            def head_transpose(J):
                wait(pe, head_Tcopy, J - 3)
                for tt in range(TT):
                    n = TT * J + tt
                    if n < XN_POOL[0]:
                        pe.wait_ge(xn_dve, n + 1)
                    elif n < XN_POOL[1]:
                        pe.wait_ge(xn_pool, n - XN_POOL[0] + 1)
                    else:
                        pe.wait_ge(xn_dve, n - (XN_POOL[1] - XN_POOL[0]) + 1)
                    for kd in range(KD):
                        ins = nc.tensor.transpose(hs_bank(J)[:, kd * T + tt * P:kd * T + tt * P + P],
                                                  xn_all[:, TT * J + tt, kd * P:kd * P + P], ident[:])
                ins.then_inc(head_T, 1)

            def merge(jt):
                wait(pe, wm_free, jt - 1)
                for it in range(CT):
                    ins = nc.tensor.matmul((m0, m1)[jt % 2][:], xw_tmp[:, it, P * jt:P * jt + P], dtw_tmp[:, it, :],
                                           start=(it == 0), stop=(it == CT - 1))
                ins.then_inc(wm_full, 1)

            def logits(n):
                pe.wait_ge(head_Tcopy, n // TT + 1)
                if n == 0:
                    pe.wait_ge(wm_free, CT)
                for kd in range(KD):
                    ins = nc.tensor.matmul(m1[:, E * n:E * n + E],
                                           xnT_all[:, n // TT, kd, P * (n % TT):P * (n % TT) + P],
                                           gw[:, kd, :], start=(kd == 0), stop=(kd == KD - 1))
                ins.then_inc(gate_done, 1)

            def prefixes():
                pe.wait_ge(mask_ready, 1)
                mask = w1s_flat[:, 5 * D:5 * D + NT * E]
                nc.tensor.matmul(m0[:, 0:256], upper, mask, start=True, stop=True)
                nc.tensor.matmul(m0[:, 256:512], ones, mask, start=True, stop=True).then_inc(prefix_ready, 1)

            def in_proj(J, r, m):
                wait(pe, pj_free, pj_ahead(J, r))
                rows = xnT
                if isinstance(J, int) and J == 0:
                    rows = xnT_all[:, 0]
                elif m == 0:
                    pe.wait_ge(xnT_in, 16 * J)
                for j in range(2):
                    for kd in range(KD):
                        ins = nc.tensor.matmul(pj[:, T * j:T * j + T], w_in[:, kd, P * (m + j):P * (m + j + 1)],
                                               rows[:, kd, :], start=(kd == 0), stop=(kd == KD - 1))
                ins.then_inc(pj_full, 1)

            def delta_proj(J, ci, pair):
                wait(pe, pj_free, pj_ahead(J, PJ_DT + pair))
                if pair == 0:
                    pe.wait_ge(xin_ready, CT * (J + 1))
                for j in range(2):
                    e0 = P * (2 * pair + j)
                    for c in range(CT):
                        ins = nc.tensor.matmul(pj[:, T * j:T * j + T], w_dt[:, c, e0:e0 + P], xin[:, ci, c, :],
                                               start=(c == 0), stop=(c == CT - 1))
                ins.then_inc(pj_full, 1)

            def bc_proj(J, ci):
                wait(pe, pj_free, pj_ahead(J, PJ_BC))
                for c in range(CT):
                    ins = nc.tensor.matmul(pj[:, 0:T], w_bc[:, c, :], xin[:, ci, c, :],
                                           start=(c == 0), stop=(c == CT - 1))
                ins.then_inc(pj_full, 1)

            def spread(J, q, i, other=None):
                wait(pe, pj_free, spread_use(J, q, i) - (1 if other is not None and i > 0 else 0))
                for j in range(2):
                    row = S * (i // 2) + SQ * q + 2 * (i % 2) + j
                    ins = nc.tensor.matmul(spread_bank(other, i)[:, T * j:T * j + T],
                                           pick[:, row:row + 1].broadcast_to([P, P]), bcr[:],
                                           start=True, stop=True)
                ins.then_inc(pj_full, 1)

            def out_proj(J, ci):
                wait(pe, pj_free, pj_index(J + 1, PJ_OUT))
                pe.wait_ge(gated, CT * (J + 1))
                for tt in range(TT):
                    for c in range(CT):
                        ins = nc.tensor.matmul(pj[:, D * tt:D * tt + D], gz[:, ci, c, P * tt:P * tt + P],
                                               w_out[:, c, :],
                                               start=(c == 0), stop=(c == CT - 1))
                ins.then_inc(pj_full, 1)

            def sum_states(g, kk, folded):
                K = GS * g + kk
                q = kk % NQ
                if folded:
                    pe.wait_ge(quarter_done, K - FOLD_FROM + 1)
                else:
                    pe.wait_ge(mul_done, K + 1)
                if q == 0:
                    wait(pe, y_skip, 2 * CT * g + kk // NQ)
                n = 1 if folded else 4
                for j in range(n):
                    src = half[:, kk % 4, T * j:T * j + T] if folded else prod[:, kk % 2, T * j:T * j + T]
                    ins = nc.tensor.matmul(ysum[:, 0:T], ident[:], src,
                                           start=(q == 0 and j == 0), stop=(q == NQ - 1 and j == n - 1))
                ins.then_inc(sum_done, 1)

            def block_T(g, m):
                slot = GM * (g - 1) + m
                pe.wait_ge(xs_in[m % 3], 16 * (4 * (g - 1) + m // 3 + 1))
                pe.wait_ge(h_act, 2 * slot + 2)
                for kd in range(KD):
                    ins = nc.tensor.transpose(bank(m, "T")[:, P * kd:P * kd + P], xs[:, m % 3, P * kd:P * kd + P],
                                              ident[:])
                ins.then_inc(xsT_full, 1)

            def block_h(g, m, i):
                slot = GM * (g - 1) + m
                hf = i // 2
                if i == 0:
                    pe.wait_ge(xsT_ready, slot + 1)
                if i == 2:
                    pe.wait_ge(y_ready, slot + 1)
                hi = 2 * m + hf
                if i % 2 == 0:
                    pe.wait_ge(w1_in[hi % 3], 16 * (8 * (g - 1) + hi // 3 + 1))
                for f in (2 * (i % 2), 2 * (i % 2) + 1):
                    for kd in range(KD):
                        ins = nc.tensor.matmul(bank(m, hf)[:, P * f:P * f + P], w1s[:, hi % 3, kd, P * f:P * f + P],
                                               xsT[:, kd, :], start=(kd == 0), stop=(kd == KD - 1))
                if i % 2 == 1:
                    ins.then_inc(h_full, 1)

            def block_y(g, m, i, e):
                slot = GM * (g - 1) + m
                if m == 0 and i == 0:
                    pe.wait_ge(w2_load, 16 * E)
                if i % 2 == 0:
                    pe.wait_ge(h_act, 2 * slot + 3 + i // 2)
                for f in (2 * i, 2 * i + 1):
                    ins = nc.tensor.matmul(bank(m, "y")[:, 0:D], hT[:, f, :], w2s[:, bass.ds(e * (FT * D) + f * D, D)],
                                           start=(f == 0), stop=(f == FT - 1))
                if i == 3:
                    ins.then_inc(y_full, 1)

            def block_quarter(g, kk, i, e):
                for m in range(GM):
                    if kk == H_AT[m]:
                        block_h(g, m, i)
                    if kk == H_AT[m] + 1:
                        block_y(g, m, i, e)

            pe.wait_ge(w_merge, 32)
            for jt in range(CT):
                merge(jt)
            pe.wait_ge(const_ready, N_CONST)
            pe.wait_ge(w_first, 32)
            head_transpose(0)
            head_transpose(1)
            pe.wait_ge(head_Tcopy, 1)
            in_proj(0, PJ_X, 0)
            head_transpose(2)
            in_proj(0, PJ_X + 1, 2)
            head_transpose(3)
            in_proj(0, PJ_Z, 4)
            head_transpose(4)
            in_proj(0, PJ_Z + 1, 6)
            for J in range(5, 8):
                head_transpose(J)
            pe.wait_ge(w_load, 16 * N_W)
            delta_proj(0, 0, 0)
            head_transpose(8)
            head_transpose(9)
            delta_proj(0, 0, 1)
            head_transpose(10)
            head_transpose(11)
            bc_proj(0, 0)
            head_transpose(12)
            pe.wait_ge(pick_ready, 1)
            pe.wait_ge(wm_free, CT)
            pe.wait_ge(pj_free, pj_ahead(0, PJ_BC) + 1)
            for i in range(8):
                spread(0, i // 4, i % 4, m0)
                if i < 3:
                    head_transpose(13 + i)
                logits(i)

            def body(g, first=False, last=False):
                blocks = not (first or last)
                for kk in range(GS):
                    ci, k = kk // STEPS, kk % STEPS
                    J = 2 * g + ci
                    prep = not (last and ci == 1)
                    e = None
                    if blocks:
                        for m in range(GM):
                            if kk == H_AT[m] + 1:
                                e = pe.value_load(slot_e[0:1, bass.ds(GM * (g - 1) + m, 1)], min_val=0, max_val=E - 1)
                    if first and kk == CHOOSE_AT + 1:
                        prefixes()
                    if blocks and kk + 1 in H_AT:
                        block_T(g, H_AT.index(kk + 1))
                    if kk == GS - 1 and not last:
                        block_T(g + 1, 0)
                    if prep and k in X_AT:
                        in_proj(J + 1, PJ_X + X_AT.index(k), 2 * X_AT.index(k))
                    if k == OUT_AT and not (first and ci == 0):
                        out_proj(J - 1, 1 - ci)
                    if prep and k in Z_AT:
                        in_proj(J + 1, PJ_Z + Z_AT.index(k), 4 + 2 * Z_AT.index(k))
                    if prep and k in DELTA_AT:
                        delta_proj(J + 1, 1 - ci, DELTA_AT.index(k))
                    if prep and k == BC_AT:
                        bc_proj(J + 1, 1 - ci)
                    for i in range(4):
                        if first and kk <= CHOOSE_AT:
                            if 8 + 4 * kk + i < NT:
                                logits(8 + 4 * kk + i)
                        other = None if blocks else m0 if first and ci == 0 and k < 2 else m1
                        if last and kk == 0 and i == 1:
                            pe.wait_ge(y_ready, SLOTS + 1)
                        if k < 2:
                            spread(J, 2 + k, i, other)
                        if prep and k >= 14:
                            spread(J + 1, k - 14, i, other)
                        if blocks:
                            block_quarter(g, kk, i, e)
                    if blocks:
                        if kk < 3:
                            sum_states(g - 1, kk - 3 + GS, True)
                        else:
                            sum_states(g, kk - 3, True)
                    if first:
                        if 1 <= kk <= FOLD_FROM:
                            sum_states(g, kk - 1, False)
                        if kk - 3 >= FOLD_FROM:
                            sum_states(g, kk - 3, True)
                    if last:
                        if kk == 0:
                            sum_states(g - 1, GS - 3, True)
                            sum_states(g - 1, GS - 2, True)
                        if kk == 1:
                            sum_states(g - 1, GS - 1, True)
                        if kk >= 1:
                            sum_states(g, kk - 1, False)

            pe.sem_inc(h_full, 2)
            pe.sem_inc(y_full, 1)
            body(0, first=True)
            with pe.Fori(1, GROUPS - 1) as g:
                body(g)
            body(GROUPS - 1, last=True)
            sum_states(GROUPS - 1, GS - 1, False)
            out_proj(NCH - 1, 1)


_INS = {
    "x": (L, D), "in_wT": (D, 2 * DI), "conv_w": (DI, 1, TAPS), "conv_b": (DI,), "xp_w": (DI, DI),
    "bc_wT": (DI, 2 * S), "dt_wT": (DI, DI), "dt_b": (DI,), "A_log": (DI, S), "D_skip": (DI,),
    "out_wT": (DI, D), "gate_w": (D, E), "w1": (2 * E, P, KD * HF), "w2": (E, P, FT * D),
}


def kernel(L0_attn_x, L0_attn_in_proj_w, L0_attn_conv_w, L0_attn_conv_b, L0_attn_x_proj_w, L0_attn_dt_proj_w,
           L0_attn_dt_proj_b, L0_attn_A_log, L0_attn_D, L0_attn_out_proj_w, L0_ffn_gate_w, L0_ffn_w1, L0_ffn_w2):
    import concourse.bacc as bacc
    from concourse.bass_utils import run_bass_kernel_spmd

    w1 = np.asarray(L0_ffn_w1).reshape(E, KD, P, 2, HF).transpose(0, 3, 2, 1, 4).reshape(2 * E, P, KD * HF)
    w2 = np.asarray(L0_ffn_w2).reshape(E, FT, P, D).transpose(0, 2, 1, 3).reshape(E, P, FT * D)
    xp = np.asarray(L0_attn_x_proj_w)
    arrays = {
        "x": np.asarray(L0_attn_x).reshape(L, D), "in_wT": np.asarray(L0_attn_in_proj_w).T,
        "conv_w": L0_attn_conv_w, "conv_b": L0_attn_conv_b, "xp_w": xp[:DI], "bc_wT": xp[DI:].T,
        "dt_wT": np.asarray(L0_attn_dt_proj_w).T, "dt_b": L0_attn_dt_proj_b, "A_log": L0_attn_A_log,
        "D_skip": L0_attn_D, "out_wT": np.asarray(L0_attn_out_proj_w).T, "gate_w": L0_ffn_gate_w, "w1": w1, "w2": w2,
    }
    arrays = {k: np.ascontiguousarray(a) for k, a in arrays.items()}
    nc = bacc.Bacc("TRN2", target_bir_lowering=False, num_devices=1)
    aps = [nc.dram_tensor(k, shape, F32, kind="ExternalInput").ap() for k, shape in _INS.items()]
    out = nc.dram_tensor("out", (L, D), F32, kind="ExternalOutput").ap()
    mamba_moe_kernel(nc, *aps, out)
    r = run_bass_kernel_spmd(nc, [arrays], core_ids=[0])
    return r.results[0]["out"].reshape(1, L, D)
```
